# Optimizing a Trainium2 kernel written in Bass

```python
import numpy as np
import jax
import jax.numpy as jnp

def _softmax(x, axis=-1):
    return jax.nn.softmax(x, axis=axis)
def _gelu(x):
    return jax.nn.gelu(x, approximate=True)
def _silu(x):
    return jax.nn.silu(x)
def _sigmoid(x):
    return jax.nn.sigmoid(x)
def _layernorm(x, axis=-1, eps=1e-5):
    m = jnp.mean(x, axis=axis, keepdims=True)
    v = jnp.var(x, axis=axis, keepdims=True)
    return (x - m) / jnp.sqrt(v + eps)
def _scatter_add(tgt, idx, src, axis=0):
    return tgt.at[idx].add(src)
def _segment_sum(src, seg, n):
    return jax.ops.segment_sum(src, seg, n)

kernel_name = 'mk_metaformer_d1_conv_nchw128_2e8c0a'

def setup_inputs(seed: int = 0):
    np.random.seed(seed)
    _w = jnp.asarray
    def _rec_inputs():
        import jax
        import jax.numpy as jnp
        _gk = jax.random.key(seed)
        x = -0.000125 + 0.9999 * jax.random.normal(jax.random.fold_in(_gk, 1), (16, 128, 128, 128), jnp.float32)
        return x
    x = _rec_inputs()
    def _L0_conv_setup():
        import jax, jax.numpy as jnp
        import numpy as np
        key = jax.random.key(seed)
        k1, k2 = jax.random.split(key)
        B, C, H, W = (16, 128, 128, 128)
        x = jax.random.normal(k1, (B, C, H, W), dtype=jnp.float32)
        w = jax.random.normal(k2, (C, C), dtype=jnp.float32) * (1.0 / np.sqrt(C))
        return {'x': x, 'w': w}
    _L0_conv_all = _L0_conv_setup()
    _L0_conv_in = {k: v for k, v in _L0_conv_all.items() if k in ('w', )}
    del _L0_conv_all

    def _L0_ffn_setup():
        import jax, jax.numpy as jnp
        import numpy as np
        B, S, D, E, H, O, K = (512, 2048, 128, 64, 512, 128, 8)
        key = jax.random.key(seed)
        k0, k1, k2, k3 = jax.random.split(key, 4)
        x = jax.random.normal(k0, (B, S, D), dtype=jnp.float32)
        gate_w = jax.random.normal(k1, (E, D), dtype=jnp.float32) * (1.0 / np.sqrt(D))
        gate_b = jnp.zeros((E,), dtype=jnp.float32)
        weight1 = jax.random.uniform(k2, (E, D + 1, H), dtype=jnp.float32, minval=-1.0, maxval=1.0) * (1.0 / np.sqrt(D + 1))
        weight2 = jax.random.uniform(k3, (E, H + 1, O), dtype=jnp.float32, minval=-1.0, maxval=1.0) * (1.0 / np.sqrt(H + 1))
        return {'x': x, 'gate_w': gate_w, 'gate_b': gate_b, 'weight1': weight1, 'weight2': weight2}
    _L0_ffn_all = _L0_ffn_setup()
    _L0_ffn_in = {k: v for k, v in _L0_ffn_all.items() if k in ('gate_w', 'gate_b', 'weight1', 'weight2', )}
    del _L0_ffn_all

    return {
        "x": x,
        "L0_conv_w": _L0_conv_in["w"],
        "L0_ffn_gate_w": _L0_ffn_in["gate_w"],
        "L0_ffn_gate_b": _L0_ffn_in["gate_b"],
        "L0_ffn_weight1": _L0_ffn_in["weight1"],
        "L0_ffn_weight2": _L0_ffn_in["weight2"],
    }

def reference(x, L0_conv_w, L0_ffn_gate_w, L0_ffn_gate_b, L0_ffn_weight1, L0_ffn_weight2):
    import jax
    import jax.numpy as jnp
    def _L0_conv_ref(x, w):
        import jax, jax.numpy as jnp
        import numpy as np
        B, C, H, W = x.shape
        N = H * W
        xf = x.reshape(B, C, N)
        gram = jnp.einsum('bcn,bdn->bcd', xf, xf) / N
        y = jnp.einsum('bcd,bdn->bcn', gram, xf)
        y = y.reshape(B, C, H, W)
        out = jnp.einsum('oc,bchw->bohw', w, y)
        return out

    def _L0_ffn_ref(x, gate_w, gate_b, weight1, weight2):
        import jax, jax.numpy as jnp
        import numpy as np
        B, S, D, E, H, O, K = (512, 2048, 128, 64, 512, 128, 8)
        Bn, Sn, Dn = x.shape
        logits = jnp.einsum('bsd,ed->bse', x, gate_w) + gate_b
        probs = jax.nn.softmax(logits, axis=1)
        vals, idx = jax.lax.top_k(probs.transpose(0, 2, 1), K)
        topv = vals.transpose(0, 2, 1)
        topi = idx.transpose(0, 2, 1)
        flat_idx = topi.reshape(Bn, K * E)
        gathered = jnp.take_along_axis(x, flat_idx[:, :, None], axis=1)
        gathered = gathered.reshape(Bn, K, E, Dn)
        pooled = jnp.einsum('bked,bke->bed', gathered, topv)
        ones = jnp.ones((E, Bn, 1), dtype=x.dtype)
        h = jnp.concatenate([pooled.transpose(1, 0, 2), ones], axis=-1)
        h = jax.nn.gelu(jnp.einsum('ebd,edh->ebh', h, weight1), approximate=False)
        h = jnp.concatenate([h, ones], axis=-1)
        out = jnp.einsum('ebh,eho->ebo', h, weight2)
        out = out.transpose(1, 0, 2)
        weighted = jnp.einsum('beo,bke->bkeo', out, topv).reshape(Bn, K * E, O)
        outputs = jnp.zeros((Bn, Sn, O), dtype=x.dtype)
        outputs = outputs.at[jnp.arange(Bn)[:, None], flat_idx].add(weighted)
        return outputs

    def _gn(v, G=32, eps=1e-5):
        B_, C_, H_, W_ = v.shape
        g = v.reshape(B_, G, C_ // G, H_, W_)
        m = jnp.mean(g, axis=(2, 3, 4), keepdims=True)
        s = jnp.var(g, axis=(2, 3, 4), keepdims=True)
        return ((g - m) / jnp.sqrt(s + eps)).reshape(v.shape)

    def _ln_c(v, eps=1e-6):
        m = jnp.mean(v, axis=1, keepdims=True)
        s = jnp.var(v, axis=1, keepdims=True)
        return (v - m) / jnp.sqrt(s + eps)

    def _ln_t(v, eps=1e-5):
        m = jnp.mean(v, axis=-1, keepdims=True)
        s = jnp.var(v, axis=-1, keepdims=True)
        return (v - m) / jnp.sqrt(s + eps)

    def _to_tokens(v):
        B_, C_, H_, W_ = v.shape
        return v.reshape(B_, C_, H_ * W_).transpose(0, 2, 1)
    def _from_tokens(t, like):
        B_, C_, H_, W_ = like.shape
        return t.transpose(0, 2, 1).reshape(B_, C_, H_, W_)

    x = x + _L0_conv_ref(_ln_c(x), L0_conv_w)
    t = _to_tokens(x)
    t = t + _L0_ffn_ref(_ln_t(t), L0_ffn_gate_w, L0_ffn_gate_b, L0_ffn_weight1, L0_ffn_weight2)
    x = _from_tokens(t, x)
    return x


_drawn_inputs = setup_inputs


def setup_inputs(seed=0):
    import zlib

    import numpy as np

    out = dict(_drawn_inputs(seed))
    spreads = {'L0_ffn_gate_b': (0.0, 0.1)}
    factors = {'L0_ffn_gate_w': 8.0, 'L0_ffn_weight1': 8.0, 'L0_ffn_weight2': 8.0}
    for name, (base, spread) in spreads.items():
        noise = np.random.default_rng([zlib.crc32(name.encode()), seed]).standard_normal(out[name].shape)
        drawn = base * np.exp(spread * noise) if base else spread * noise
        out[name] = jnp.asarray(drawn.astype(out[name].dtype))
    for name, factor in factors.items():
        out[name] = (out[name] * factor).astype(out[name].dtype)
    return out
```

```python
import concourse.bass as bass
from concourse import mybir
from contextlib import ExitStack

B, C, N = 16, 128, 128 * 128
E, H, O, K = 64, 512, 128, 8
HALF = N // 2
T = 128
IH = 4
GT = 2 * IH
NG = N // (GT * T)
NC = 2 * NG
XP = 8
XW = HALF // XP
TAIL = 8
HC = H // 128
EQ = 4
NJ = 4
JT = HALF // NJ
FREE = 1
NQ = 8


def build(nc, x, conv_w, gate_w, gate_b, w1, w2, out):
    f32, bf16, u32 = mybir.dt.float32, mybir.dt.bfloat16, mybir.dt.uint32
    ALU, ACT, AX = mybir.AluOpType, mybir.ActivationFunctionType, mybir.AxisListType

    tok = nc.dram_tensor("tok_scratch", (B, 2, T, N // (2 * T), C), f32, kind="Internal").ap()
    prob = nc.dram_tensor("prob_scratch", (B, 128, HALF), f32, kind="Internal").ap()
    eout = nc.dram_tensor("eout_scratch", (B, E, O), f32, kind="Internal").ap()
    cur = nc.dram_tensor("cur_scratch", (2, T, N // (2 * T), C), f32, kind="Internal").ap()
    cur_rows = cur.rearrange("h p t c -> (h p t) c")

    ctx = ExitStack()
    with ctx:
        def sb(name, shape, dt=f32):
            return ctx.enter_context(nc.sbuf_tensor(name, shape, dt))

        def sem(name):
            return ctx.enter_context(nc.semaphore(name))

        bank = [ctx.enter_context(nc.psum_tensor(f"bank{i}", [128, 512], f32)) for i in range(8)]

        X = sb("X", [128, 2, HALF])
        P = sb("P", [128, HALF + TAIL])
        hit = sb("hit", [128, HALF + TAIL], bf16)
        ident = sb("ident", [128, 128])
        fold = sb("fold", [128, E])
        convT = sb("convT", [128, 128])
        gwT = sb("gwT", [128, E])
        gb = sb("gb", [128, 1])
        ones = sb("ones", [1, B])
        mhalf = sb("mhalf", [128, GT])
        quarter = sb("quarter", [128, GT])
        wsel = sb("wsel", [128, K])
        row0 = sb("row0", [128, 1])
        zT = sb("zT", [128, 2, GT, 128])
        yT = sb("yT", [128, 2, 512])
        x2T = sb("x2T", [128, 4, 2, IH, 128])
        x2 = sb("x2", [128, 2, 512])
        Ls = sb("Ls", [128, 2, IH, 2, E])
        st = sb("st", [128, 2, GT, 6])
        r1 = sb("r1", [128, NG * GT])
        nmr1 = sb("nmr1", [128, NG * GT])
        r2 = sb("r2", [128, 2, GT])
        gram = sb("gram", [128, 128])
        BT = sb("BT", [128, 128])
        pt = sb("pt", [128, 8, GT])
        cand = sb("cand", [128, NG * 8])
        top = sb("top", [128, 8])
        candm = sb("candm", [64, 16])
        e16 = sb("e16", [64, 16])
        rep16 = sb("rep16", [64, 16])
        selm = sb("selm", [64, 16])
        u8 = sb("u8", [64, 8])
        sel = sb("sel", [128, 8])
        negmax = sb("negmax", [128, 1])
        esum = sb("esum", [128, 1])
        es = sb("es", [64, 2])
        sinv = sb("sinv", [128, B])
        inv = sb("inv", [128, 1])
        idx = sb("idx", [128, 8], u32)
        ia = sb("ia", [128, 8], u32)
        ib = sb("ib", [128, 8], u32)
        rows = sb("rows", [128, 8], u32)
        G = sb("G", [128, K, 128])
        stg = sb("stg", [128, K, 6])
        rw = sb("rw", [128, K])
        nmrw = sb("nmrw", [128, K])
        U = sb("U", [128, K, 128])
        pooled = sb("pooled", [128, B, E])
        W1s = sb("W1s", [128, EQ, H])
        W1bs = sb("W1bs", [1, EQ, H])
        W2s = sb("W2s", [128, EQ, HC, O])
        W2bs = sb("W2bs", [1, EQ, O])
        Xf = X[:, :, :].rearrange("p h n -> p (h n)")
        Pf = P[:, 0:HALF]
        W1 = [W1s[:, :, :], Xf[:, 4096:6144].rearrange("p (e h) -> p e h", e=EQ)]
        W2 = [W2s[:, :, :, :], Xf[:, 6144:8192].rearrange("p (e a o) -> p e a o", e=EQ, a=HC)]
        W1b = [W1bs[:, :, :], Xf[0:1, 8192:10240].rearrange("p (e h) -> p e h", e=EQ)]
        W2b = [W2bs[:, :, :], Xf[0:1, 10240:10752].rearrange("p (e o) -> p e o", e=EQ)]
        hT = [Xf[:, s * 256:(s + 1) * 256].rearrange("p (e h b) -> p e h b", e=EQ, h=HC) for s in range(2)]
        Osb = [Xf[0:B, 512 + s * 512:1024 + s * 512] for s in range(2)]
        O2 = Xf[:, 14336:16384].rearrange("p (b o) -> p b o", b=B)
        xin = [Pf[:, s * 4096:(s + 1) * 4096].rearrange("p (h t c) -> p h t c", h=2, c=C) for s in range(2)]
        pin = [Xf[:, s * 2048:(s + 1) * 2048] for s in range(2)]
        osb = [Xf[:, 4096 + s * 4096:8192 + s * 4096].rearrange("p (h n) -> p h n", h=2) for s in range(2)]
        Ob = [Xf[:, 12288 + s * 128:12416 + s * 128] for s in range(2)]

        s_const = sem("s_const")
        s_ident = sem("s_ident")
        s_small = sem("s_small")
        s_gwc = sem("s_gwc")
        s_tr0 = sem("s_tr0")
        s_prep = sem("s_prep")
        x_loaded = [sem(f"x_loaded{j}") for j in range(XP)]
        xT_ready = sem("xT_ready")
        st1_ready = sem("st1_ready")
        norm1_ready = sem("norm1_ready")
        z_ready = sem("z_ready")
        gram_done = sem("gram_done")
        gram_copied = sem("gram_copied")
        bt_done = sem("bt_done")
        bt_copied = sem("bt_copied")
        y_ready = sem("y_ready")
        yT_ready = sem("yT_ready")
        x2T_ready = sem("x2T_ready")
        x2_tr = sem("x2_tr")
        x2_ready = sem("x2_ready")
        logit_done = sem("logit_done")
        st2_ready = sem("st2_ready")
        norm2_ready = sem("norm2_ready")
        lscaled = sem("lscaled")
        lT_done = sem("lT_done")
        l_ready = sem("l_ready")
        x2T_stored = [sem(f"x2T_stored{s}") for s in range(4)]
        negmax_ready = sem("negmax_ready")
        exp_ready = sem("exp_ready")
        p_ready = sem("p_ready")
        p_stored = sem("p_stored")
        rows_ready = sem("rows_ready")
        gathered = sem("gathered")
        stg_ready = sem("stg_ready")
        normg_ready = sem("normg_ready")
        u_ready = sem("u_ready")
        pool_done = sem("pool_done")
        pooled_ready = sem("pooled_ready")
        dve_step = sem("dve_step")
        cand_done = sem("cand_done")
        u8_done = sem("u8_done")
        sel_done = sem("sel_done")
        pool_step = sem("pool_step")
        w_loaded = [sem(f"w_loaded{s}") for s in range(2)]
        up_done = [sem(f"up_done{s}") for s in range(2)]
        gelu_done = [sem(f"gelu_done{s}") for s in range(2)]
        down_done = [sem(f"down_done{s}") for s in range(2)]
        o_ready = [sem(f"o_ready{s}") for s in range(2)]
        o_stored = [sem(f"o_stored{s}") for s in range(2)]
        o2_loaded = sem("o2_loaded")
        o2_ready = sem("o2_ready")
        ob_ready = sem("ob_ready")
        blk_loaded = [sem(f"blk_loaded{s}") for s in range(2)]
        blk_used = [sem(f"blk_used{s}") for s in range(2)]
        sc_done = sem("sc_done")
        ev = [sem(f"ev{q}") for q in range(NQ)]
        out_stored = [sem(f"out_stored{s}") for s in range(2)]

        DVE_STEPS = 13
        POOL_STEPS = NG * 9 + 6

        block = ctx.enter_context(nc.Block())

        def xtile(k, h, i):
            return X[:, h, (k * IH + i) * T:(k * IH + i + 1) * T]

        start_free = [gram_done, lT_done, l_ready, logit_done, lscaled, norm1_ready, norm2_ready, p_stored, pool_done, pooled_ready, x2T_ready, x2_ready, x2_tr, yT_ready, z_ready,
                      *x2T_stored, *down_done, *o_stored, *gelu_done, *o_ready, *ev, *blk_used, *out_stored]

        @block.sync
        def _(sp):
            for semaphore in start_free:
                sp.sem_inc(semaphore, FREE)
            sp.dma_start(gram[:, :], conv_w).then_inc(s_small, 16)
            sp.dma_start(BT[0:E, :], gate_w).then_inc(s_small, 16)
            for h in range(2):
                sp.dma_start(gb[h * E:(h + 1) * E, :], gate_b.rearrange("(e a) -> e a", a=1)).then_inc(s_small, 16)

            def load_x(b, j):
                src = x[b].rearrange("c (h n) -> c h n", h=2)
                sp.dma_start(X[:, :, j * XW:(j + 1) * XW], src[:, :, j * XW:(j + 1) * XW]).then_inc(x_loaded[j], 16)

            def load_w(q, s):
                e = q * EQ
                sp.dma_start(W1[s], w1[bass.ds(e, EQ), 0:C, :].rearrange("e c h -> c e h")).then_inc(w_loaded[s], 16)
                sp.dma_start(W1b[s], w1[bass.ds(e, EQ), C:C + 1, :].rearrange("e c h -> c e h")).then_inc(w_loaded[s], 16)
                for i in range(EQ):
                    sp.dma_start(W2[s][:, i], w2[e + i, 0:H, :].rearrange("(a p) o -> p a o", p=128)).then_inc(w_loaded[s], 16)
                sp.dma_start(W2b[s], w2[bass.ds(e, EQ), H:H + 1, :].rearrange("e c h -> c e h")).then_inc(w_loaded[s], 16)

            for j in range(XP):
                load_x(0, j)
            load_w(0, 0)

            def image(b, more):
                for k in range(NG):
                    sp.wait_ge(x2T_ready, b * NC + 2 * k + 2 + FREE)
                    sp.dma_start(tok[b, :, :, k * IH:(k + 1) * IH, :].rearrange("h p t c -> p h t c"),
                                 x2T[:, k % 4]).then_inc(x2T_stored[k % 4], 16)
                    if k == 0:
                        sp.wait_ge(pooled_ready, b + FREE)
                    sp.dma_start(cur[:, :, k * IH:(k + 1) * IH, :].rearrange("h p t c -> p h t c"),
                                 x2T[:, k % 4]).then_inc(x2T_stored[k % 4], 16)
                    if more and k % 2 == 1:
                        sp.wait_ge(y_ready, b * NC + 2 * k + 2)
                        load_x(b + 1, k // 2)
                sp.wait_ge(p_ready, b + 1)
                sp.dma_start(prob[b], P[:, 0:HALF]).then_inc(p_stored, 16)

            with sp.Fori(0, B - 1) as b:
                image(b, True)
            image(B - 1, False)
            sp.wait_ge(y_ready, B * NC)
            load_w(1, 1)

            def store_o(kk, s):
                sp.wait_ge(o_ready[s], kk + 1 + FREE)
                q = kk * 2 + s
                sp.dma_start(eout[:, bass.ds(q * EQ, EQ), :], Osb[s].rearrange("b (e o) -> b e o", o=O)).then_inc(o_stored[s], 16)

            with sp.Fori(0, E // EQ // 2 - 1) as kk:
                for s in range(2):
                    store_o(kk, s)
                    sp.wait_ge(down_done[s], kk + 1 + FREE)
                    load_w(kk * 2 + 2 + s, s)
            for s in range(2):
                store_o(E // EQ // 2 - 1, s)
            for s in range(2):
                sp.wait_ge(o_stored[s], 16 * (E // EQ // 2) + FREE)
            for h in range(2):
                sp.dma_start(O2[h * E:(h + 1) * E], eout.rearrange("b e o -> e b o")).then_inc(o2_loaded, 16)

            sp.wait_ge(p_stored, 16 * B + FREE)
            for s in range(4):
                sp.wait_ge(x2T_stored[s], 32 * B * NG // 4 + FREE)
            with sp.Fori(0, B) as b:
                for j in range(NJ):
                    s = j % 2
                    sp.wait_ge(blk_used[s], b * (NJ // 2) + j // 2 + FREE)
                    sp.dma_start(xin[s], tok[b, :, :, j * (JT // T):(j + 1) * (JT // T), :].rearrange("h p t c -> p h t c")
                                 ).then_inc(blk_loaded[s], 16)
                    sp.dma_start(pin[s], prob[b, :, j * JT:(j + 1) * JT]).then_inc(blk_loaded[s], 16)

        @block.gpsimd
        def _(pool):
            pool.memset(ident[:, :], 0.0).then_inc(s_ident, 1)
            pool.memset(fold[:, :], 0.0).then_inc(s_ident, 1)
            pool.wait_ge(s_ident, 2)
            pool.affine_select(out=ident[:, :], in_=ident[:, :], compare_op=ALU.not_equal, fill=1.0, base=0,
                               pattern=[[-1, 128]], channel_multiplier=1).then_inc(s_ident, 1)
            pool.affine_select(out=fold[:, :], in_=fold[:, :], compare_op=ALU.not_equal, fill=1.0, base=0,
                               pattern=[[-1, E]], channel_multiplier=1).then_inc(s_ident, 1)
            pool.wait_ge(s_ident, 4)
            pool.affine_select(out=fold[:, :], in_=fold[:, :], compare_op=ALU.not_equal, fill=1.0, base=-E,
                               pattern=[[-1, E]], channel_multiplier=1).then_inc(s_const, 1)
            pool.memset(mhalf[:, :], -0.5)
            pool.memset(quarter[:, :], 0.25).then_inc(s_const, 1)
            pool.memset(P[:, HALF:HALF + TAIL], 0.0).then_inc(s_const, 1)
            pool.memset(row0[:, :], float(HALF)).then_inc(s_const, 1)
            pool.memset(ones[:, :], 1.0).then_inc(s_const, 1)
            pool.wait_ge(s_const, 5)
            pool.memset(row0[0:E, :], 0.0).then_inc(s_const, 1)
            pool.wait_ge(s_const, 6)

            def image(b):
                n = [0]
                imgs = pool.snap(b + 1)
                stored = pool.snap(b * (NG // 4 * 32) + NG // 4 * 32 + FREE)

                def settle(ins):
                    n[0] += 1
                    ins.then_inc(pool_step, 1)
                    pool.wait_ge(pool_step, b * POOL_STEPS + n[0])

                def rsqrt(src, r, eps):
                    w = src.shape[1]
                    diff, sq, both, part, total, nmean, v = (pt[:, i, 0:w] for i in range(7))
                    pool.tensor_tensor(diff, src[:, :, 1], src[:, :, 4], ALU.subtract)
                    pool.tensor_tensor(total, src[:, :, 1], src[:, :, 4], ALU.add)
                    settle(pool.tensor_tensor(both, src[:, :, 2], src[:, :, 5], ALU.add))
                    pool.tensor_tensor(sq, diff, diff, ALU.mult)
                    pool.tensor_scalar(nmean, total, -0.5, None, ALU.mult)
                    settle(pool.tensor_scalar(part, both, 1.0 / C, eps, ALU.mult, ALU.add))
                    settle(pool.tensor_tensor(sq, sq, quarter[:, 0:w], ALU.mult))
                    settle(pool.tensor_tensor(v, sq, part, ALU.add))
                    return pool.tensor_tensor(r, v, mhalf[:, 0:w], ALU.pow)

                for k in range(NG):
                    pool.wait_ge(st1_ready, b * NG + k + 1)
                    if k == 0:
                        pool.wait_ge(yT_ready, b * NC + FREE)
                    r = r1[:, k * GT:(k + 1) * GT]
                    settle(rsqrt(st[:, k % 2], r, 1e-6))
                    pool.tensor_tensor(nmr1[:, k * GT:(k + 1) * GT], pt[:, 5, 0:GT], r, ALU.mult).then_inc(norm1_ready, 1)
                for k in range(NG):
                    pool.wait_ge(st2_ready, b * NG + k + 1)
                    pool.wait_ge(lscaled, b * NG + max(k - 1, 0) + FREE)
                    rsqrt(st[:, k % 2], r2[:, k % 2], 1e-5).then_inc(norm2_ready, 1)
                for s in range(4):
                    pool.wait_ge(x2T_stored[s], stored)
                pool.wait_ge(rows_ready, imgs)
                pool.tensor_tensor(pt[:, 7, 0:1], mhalf[:, 0:1], mhalf[:, 0:1], ALU.add)
                for i in range(K):
                    pool.indirect_dma_start(out=G[:, i, :], out_offset=None, in_=cur_rows[:, :],
                                            in_offset=bass.IndirectOffsetOnAxis(ap=rows[:, i:i + 1], axis=0),
                                            ).then_inc(gathered, 16)
                pool.wait_ge(stg_ready, b + 1)
                settle(rsqrt(stg[:, :, :], pt[:, 7, 0:K], 1e-5))
                settle(pool.tensor_tensor(rw[:, :], pt[:, 7, 0:K], wsel[:, :], ALU.mult))
                pool.tensor_tensor(nmrw[:, :], rw[:, :], pt[:, 5, 0:K], ALU.mult).then_inc(normg_ready, 1)

                assert n[0] == POOL_STEPS

            with pool.Fori(0, B) as b:
                image(b)

        @block.scalar
        def _(act):
            def image(b):
                for k in range(NG):
                    act.wait_ge(norm1_ready, b * NG + k + 1 + FREE)
                    act.wait_ge(xT_ready, b * NG + k + 1)
                    act.wait_ge(gram_done, b * NG + max(k - 1, 0) + FREE)
                    for t in range(GT):
                        h, i = t // IH, t % IH
                        c = k * GT + t
                        ins = act.activation(zT[:, k % 2, t, :], bank[2 * (k % 2) + h][:, i * 128:(i + 1) * 128],
                                             ACT.Identity, bias=nmr1[:, c:c + 1], scale=r1[:, c:c + 1])
                    ins.then_inc(z_ready, 1)
                act.wait_ge(gram_done, (b + 1) * NG + FREE)
                act.activation(gram[:, :], bank[4][:, 0:128], ACT.Copy, scale=1.0 / N).then_inc(gram_copied, 1)
                act.wait_ge(bt_done, b + 1)
                act.activation(BT[:, :], bank[5][:, 0:128], ACT.Copy).then_inc(bt_copied, 1)

                def copy_x2(g):
                    act.wait_ge(x2_tr, b * NC + g + 1 + FREE)
                    act.wait_ge(logit_done, b * NC + max(g - 1, 0) + FREE)
                    act.activation(x2[:, g % 2, :], bank[4 + g % 2][:, :], ACT.Copy).then_inc(x2_ready, 1)

                def copy_l(k):
                    act.wait_ge(lT_done, b * NG + k + 1 + FREE)
                    if k == 0:
                        act.wait_ge(p_stored, b * 16 + FREE)
                    act.activation(P[:, k * 512:(k + 1) * 512], bank[7][:, :], ACT.Identity,
                                   bias=gb[:, 0:1]).then_inc(l_ready, 1)

                for g in range(NC + 1):
                    if g < NC:
                        k, cc = g // 2, g % 2
                        act.wait_ge(y_ready, b * NC + g + 1)
                        act.wait_ge(x2T_ready, b * NC + max(g - 1, 0) + FREE)
                        for t in range(4):
                            c = k * GT + (t // 2) * IH + cc * 2 + t % 2
                            ins = act.activation(yT[:, g % 2, t * 128:(t + 1) * 128],
                                                 bank[g % 2][:, t * 128:(t + 1) * 128], ACT.Copy, scale=r1[:, c:c + 1])
                        ins.then_inc(yT_ready, 1)
                    if g >= 1:
                        copy_x2(g - 1)
                    if g >= 5 and g % 2 == 1:
                        copy_l((g - 5) // 2)
                for k in range(NG - 2, NG):
                    copy_l(k)
                act.wait_ge(negmax_ready, b + 1)
                act.activation(e16[:, :], candm[:, :], ACT.Exp, bias=negmax[0:64, 0:1])
                act.activation(P[:, 0:HALF], P[:, 0:HALF], ACT.Exp, bias=negmax[:, 0:1],
                               accum_out=esum[:, 0:1]).then_inc(exp_ready, 1)
                act.wait_ge(normg_ready, b + 1)
                act.wait_ge(pool_done, b + FREE)
                for i in range(K):
                    ins = act.activation(U[:, i, :], G[:, i, :], ACT.Identity, bias=nmrw[:, i:i + 1], scale=rw[:, i:i + 1])
                ins.then_inc(u_ready, 1)

            act.wait_ge(s_small, 64)
            act.wait_ge(s_const, 6)
            with act.Fori(0, B) as b:
                image(b)

            with act.Fori(0, E // EQ // 2) as kk:
                for s in range(2):
                    act.wait_ge(up_done[s], kk + 1)
                    act.wait_ge(down_done[s], kk + FREE)
                    act.activation(hT[s].rearrange("p e h b -> p (e h b)"), bank[s][:, 0:EQ * HC * B],
                                   ACT.Gelu).then_inc(gelu_done[s], 1)

            with act.Fori(0, B) as b:
                for j in range(NJ):
                    s = j % 2
                    act.wait_ge(out_stored[s], (b * (NJ // 2) + j // 2) * 16 + FREE)
                    for q in range(0, NQ, 2):
                        act.wait_ge(sc_done, (b * NJ + j) * (NQ - 1) + q + 1)
                        act.activation(osb[s][:, q // 4, (q % 4) * 512:(q % 4 + 1) * 512], bank[q][:, :],
                                       ACT.Copy).then_inc(ev[q], 1)
                    for q in range(NQ):
                        act.wait_ge(ev[q], b * NJ + j + 1 + FREE)
                    act.dma_start(out[b].rearrange("c (h n) -> c h n", h=2)[:, :, j * JT:(j + 1) * JT],
                                  osb[s]).then_inc(out_stored[s], 16)
            for s in range(2):
                act.wait_ge(out_stored[s], B * (NJ // 2) * 16 + FREE)

        @block.vector
        def _(dve):
            dve.wait_ge(s_small, 64)
            dve.bn_stats(st[0:E, 0, 0, :], BT[0:E, :]).then_inc(s_gwc, 1)
            dve.wait_ge(s_gwc, 1)
            dve.bn_aggr(top[0:E, 0:2], st[0:E, 0, 0, :]).then_inc(s_gwc, 1)
            dve.wait_ge(s_gwc, 2)
            dve.tensor_scalar(U[0:E, 0, :], BT[0:E, :], top[0:E, 0:1], None, ALU.subtract).then_inc(s_gwc, 1)
            dve.wait_ge(s_tr0, 1)
            dve.tensor_copy(convT[:, :], bank[0][:, 0:128]).then_inc(s_prep, 1)
            dve.tensor_copy(gwT[:, :], bank[0][:, 128:128 + E]).then_inc(s_prep, 1)

            def image(b):
                n = [0]
                turn = dve.snap(b + 1)

                def step(ins):
                    n[0] += 1
                    ins.then_inc(dve_step, 1)
                    dve.wait_ge(dve_step, b * DVE_STEPS + n[0])

                def settled(ins, semaphore):
                    ins.then_inc(semaphore, 1)
                    dve.wait_ge(s_const, 6)
                    dve.wait_ge(semaphore, turn)

                for k in range(NG):
                    dve.wait_ge(xT_ready, b * NG + k + 1)
                    dve.wait_ge(norm1_ready, b * NG + max(k - 1, 0) + FREE)
                    if k == 0:
                        dve.wait_ge(norm2_ready, b * NG + FREE)
                    for t in range(GT):
                        ins = dve.bn_stats(st[:, k % 2, t, :], bank[2 * (k % 2) + t // IH][:, (t % IH) * 128:(t % IH + 1) * 128])
                    ins.then_inc(st1_ready, 1)

                def scale_l(k):
                    dve.wait_ge(logit_done, b * NC + 2 * k + 2 + FREE)
                    dve.wait_ge(norm2_ready, b * NG + k + 1 + FREE)
                    dve.wait_ge(lT_done, b * NG + max(k - 1, 0) + FREE)
                    dve.tensor_tensor(Ls[:, k % 2].rearrange("p i h e -> p h i e"),
                                      bank[6][:, :].rearrange("p (h i e) -> p h i e", h=2, i=IH),
                                      r2[:, k % 2].rearrange("p (h i) -> p h i", h=2).unsqueeze(3).to_broadcast([128, 2, IH, E]),
                                      ALU.mult).then_inc(lscaled, 1)

                def best(k):
                    done = dve.snap(b * NG + (k + 1) + FREE)
                    dve.wait_ge(s_const, 6)
                    dve.wait_ge(l_ready, done)
                    return dve.max(cand[:, k * 8:(k + 1) * 8], P[:, k * 512:(k + 1) * 512])

                dve.wait_ge(norm1_ready, (b + 1) * NG + FREE)
                for g in range(NC):
                    k, cc = g // 2, g % 2
                    sl = k % 4
                    dve.wait_ge(yT_ready, b * NC + g + 1 + FREE)
                    dve.wait_ge(y_ready, b * NC + g + 1)
                    if cc == 0:
                        dve.wait_ge(x2T_stored[sl], (b * (NG // 4) + k // 4) * 32 + FREE)
                        dve.wait_ge(x2_tr, b * NC + max(2 * k - 6, 0) + FREE)
                        dve.wait_ge(norm2_ready, b * NG + max(k - 1, 0) + FREE)
                    dst = x2T[:, sl, :, 2 * cc:2 * cc + 2, :].rearrange("p h i c -> p h (i c)")
                    dve.tensor_tensor(dst, bank[2 + g % 2][:, :].rearrange("p (h n) -> p h n", h=2),
                                      yT[:, g % 2, :].rearrange("p (h n) -> p h n", h=2), ALU.add).then_inc(x2T_ready, 1)
                    dve.wait_ge(x2T_ready, b * NC + g + 1 + FREE)
                    for t in range(4):
                        h, i = t // 2, 2 * cc + t % 2
                        ins = dve.bn_stats(st[:, k % 2, h * IH + i, :], x2T[:, sl, h, i, :])
                    if cc == 1:
                        ins.then_inc(st2_ready, 1)
                    if cc == 1 and k >= 1:
                        scale_l(k - 1)
                    if cc == 0 and k >= 3:
                        best(k - 3)
                scale_l(NG - 1)
                for k in range(NG - 3, NG):
                    ins = best(k)
                settled(ins, cand_done)
                step(dve.max(top[:, :], cand[:, :]))
                dve.tensor_copy(candm[:, 8:16], top[64:128, :])
                step(dve.tensor_copy(candm[:, 0:8], top[0:64, :]))
                step(dve.tensor_scalar(negmax[0:64, :], candm[:, 0:1], candm[:, 8:9], -1.0, ALU.max, ALU.mult))
                dve.tensor_copy(negmax[64:128, :], negmax[0:64, :]).then_inc(negmax_ready, 1)
                dve.wait_ge(s_const, 6)
                dve.wait_ge(exp_ready, turn)
                settled(dve.max(u8[:, :], e16[:, :]), u8_done)
                step(dve.match_replace(rep16[:, :], u8[:, :], e16[:, :], 0.0))
                step(dve.tensor_tensor(selm[:, :], e16[:, :], rep16[:, :], ALU.subtract))
                dve.tensor_copy(sel[64:128, :], selm[:, 8:16])
                step(dve.tensor_copy(sel[0:64, :], selm[:, 0:8]))
                step(dve.tensor_copy(es[:, 0:1], esum[64:128, :]))
                step(dve.tensor_tensor(es[:, 1:2], es[:, 0:1], esum[0:64, :], ALU.add))
                step(dve.reciprocal(inv[0:64, :], es[:, 1:2]))
                step(dve.tensor_copy(inv[64:128, :], inv[0:64, :]))
                dve.tensor_scalar(wsel[:, :], sel[:, :], inv[:, 0:1], None, ALU.mult)
                settled(dve.tensor_copy(sinv[:, bass.ds(b, 1)], inv[:, :]), sel_done)
                step(dve.match_replace(hit[:, :], sel[:, :], P[:, :], -1.0))
                dve.scalar_tensor_tensor(P[:, :], hit[:, :], 0.0, P[:, :], ALU.is_lt, ALU.mult).then_inc(p_ready, 1)
                dve.wait_ge(s_const, 6)
                dve.wait_ge(p_ready, turn)
                step(dve.max_index(idx[:, :], sel[:, :], P[:, :]))
                dve.tensor_scalar(ia[:, :], idx[:, :], T - 1, 6, ALU.bitwise_and, ALU.logical_shift_left)
                step(dve.tensor_scalar(ib[:, :], idx[:, :], 7, None, ALU.logical_shift_right))
                dve.scalar_tensor_tensor(rows[:, :], ia[:, :], row0[:, 0:1], ib[:, :], ALU.add, ALU.add).then_inc(rows_ready, 1)
                dve.wait_ge(gathered, b * (16 * K) + 16 * K)
                for i in range(K):
                    ins = dve.bn_stats(stg[:, i, :], G[:, i, :])
                ins.then_inc(stg_ready, 1)
                dve.wait_ge(pool_done, b + 1 + FREE)
                dve.tensor_copy(pooled[:, bass.ds(b, 1), :].rearrange("p a e -> p (a e)"), bank[6][:, 0:E]).then_inc(pooled_ready, 1)

                assert n[0] == DVE_STEPS

            dve.wait_ge(s_const, 6)
            with dve.Fori(0, B) as b:
                image(b)

            with dve.Fori(0, E // EQ // 2) as kk:
                for s in range(2):
                    dve.wait_ge(down_done[s], kk + 1 + FREE)
                    dve.wait_ge(o_stored[s], kk * 16 + FREE)
                    dve.tensor_copy(Osb[s], bank[2 + s][0:B, :]).then_inc(o_ready[s], 1)
            dve.wait_ge(o2_loaded, 32)
            dve.tensor_tensor(O2, O2, sinv[:, :].unsqueeze(2).to_broadcast([128, B, O]), ALU.mult).then_inc(o2_ready, 1)
            dve.wait_ge(o2_ready, 1)
            with dve.Fori(0, B) as b:
                dve.wait_ge(blk_used[(NJ - 1) % 2], b * (NJ // 2) + FREE)
                dve.tensor_copy(Ob[0], O2[:, bass.ds(b, 1), :].rearrange("p a o -> p (a o)")).then_inc(ob_ready, 1)
                for j in range(NJ):
                    s = j % 2
                    dve.wait_ge(out_stored[s], (b * (NJ // 2) + j // 2) * 16 + FREE)
                    for q in range(1, NQ, 2):
                        if q == NQ - 1:
                            dve.wait_ge(blk_used[s], b * (NJ // 2) + j // 2 + 1 + FREE)
                        else:
                            dve.wait_ge(sc_done, (b * NJ + j) * (NQ - 1) + q + 1)
                        dve.tensor_copy(osb[s][:, q // 4, (q % 4) * 512:(q % 4 + 1) * 512], bank[q][:, :]).then_inc(ev[q], 1)

        @block.tensor
        def _(pe):
            pe.wait_ge(s_const, 6)
            pe.wait_ge(s_gwc, 3)
            pe.wait_ge(s_small, 64)
            pe.transpose(bank[0][:, 0:128], gram[:, :], ident[:, :])
            pe.transpose(bank[0][:, 128:128 + E], U[0:E, 0, :], ident[0:E, 0:E]).then_inc(s_tr0, 1)
            pe.wait_ge(s_prep, 2)

            def image(b):
                def xT_tiles(k):
                    if k % 2 == 0:
                        pe.wait_ge(x_loaded[k // 2], b * 16 + 16)
                    pe.wait_ge(z_ready, b * NG + max(k - 1, 0) + FREE)
                    for t in range(GT):
                        ins = pe.transpose(bank[2 * (k % 2) + t // IH][:, (t % IH) * 128:(t % IH + 1) * 128],
                                           xtile(k, t // IH, t % IH), ident[:, :])
                    ins.then_inc(xT_ready, 1)

                def gram_tiles(k):
                    pe.wait_ge(z_ready, b * NG + k + 1 + FREE)
                    for t in range(GT):
                        z = zT[:, k % 2, t, :]
                        ins = pe.matmul(bank[4][:, 0:128], z, z, start=(k == 0 and t == 0), stop=(k == NG - 1 and t == GT - 1))
                    ins.then_inc(gram_done, 1)

                pe.wait_ge(x2T_ready, b * NC + FREE)
                pe.wait_ge(x2_ready, b * NC + FREE)
                xT_tiles(0)
                for k in range(NG):
                    if k + 1 < NG:
                        xT_tiles(k + 1)
                    gram_tiles(k)
                pe.wait_ge(gram_copied, b + 1)
                pe.matmul(bank[5][:, 0:128], gram[:, :], convT[:, :], start=True, stop=True).then_inc(bt_done, 1)
                pe.wait_ge(bt_copied, b + 1)

                def conv(g):
                    k, cc = g // 2, g % 2
                    pe.wait_ge(yT_ready, b * NC + max(g - 1, 0) + FREE)
                    for t in range(4):
                        xt = xtile(k, t // 2, 2 * cc + t % 2)
                        pe.matmul(bank[g % 2][:, t * 128:(t + 1) * 128], xt, BT[:, :], start=True, stop=True)
                    pe.wait_ge(x2T_ready, b * NC + max(g - 1, 0) + FREE)
                    for t in range(4):
                        xt = xtile(k, t // 2, 2 * cc + t % 2)
                        ins = pe.transpose(bank[2 + g % 2][:, t * 128:(t + 1) * 128], xt, ident[:, :])
                    ins.then_inc(y_ready, 1)

                def x2_back(g):
                    k, cc = g // 2, g % 2
                    pe.wait_ge(x2T_ready, b * NC + g + 1 + FREE)
                    pe.wait_ge(x2_ready, b * NC + max(g - 1, 0) + FREE)
                    for t in range(4):
                        ins = pe.transpose(bank[4 + g % 2][:, t * 128:(t + 1) * 128],
                                           x2T[:, k % 4, t // 2, 2 * cc + t % 2, :], ident[:, :])
                    ins.then_inc(x2_tr, 1)

                def logits(g):
                    k, cc = g // 2, g % 2
                    pe.wait_ge(x2_ready, b * NC + g + 1 + FREE)
                    if cc == 0:
                        pe.wait_ge(lscaled, b * NG + k + FREE)
                        if k == 0:
                            pe.wait_ge(pooled_ready, b + FREE)
                    for t in range(4):
                        c = (t // 2) * IH + 2 * cc + t % 2
                        ins = pe.matmul(bank[6][:, c * E:(c + 1) * E], x2[:, g % 2, t * 128:(t + 1) * 128], gwT[:, :],
                                        start=True, stop=True)
                    ins.then_inc(logit_done, 1)

                def logits_T(k):
                    pe.wait_ge(lscaled, b * NG + k + 1 + FREE)
                    pe.wait_ge(l_ready, b * NG + k + FREE)
                    for i in range(IH):
                        ins = pe.transpose(bank[7][:, i * 128:(i + 1) * 128], Ls[:, k % 2, i].rearrange("p h e -> p (h e)"), ident[:, :])
                    ins.then_inc(lT_done, 1)

                for g in range(NC + 2):
                    if g < NC:
                        conv(g)
                    if 1 <= g <= NC:
                        x2_back(g - 1)
                    if g >= 4 and g % 2 == 0:
                        logits_T((g - 4) // 2)
                    if g >= 2:
                        logits(g - 2)
                logits_T(NG - 1)
                pe.wait_ge(u_ready, b + 1)
                for i in range(K):
                    ins = pe.matmul(bank[6][:, 0:E], U[:, i, :], fold[:, :], start=(i == 0), stop=(i == K - 1))
                ins.then_inc(pool_done, 1)

            with pe.Fori(0, B) as b:
                image(b)

            pe.wait_ge(pooled_ready, B + FREE)
            with pe.Fori(0, E // EQ // 2) as kk:
                for s in range(2):
                    q = kk * 2 + s
                    pe.wait_ge(w_loaded[s], kk * (16 * 7) + 16 * 7)
                    pe.wait_ge(gelu_done[s], kk + FREE)
                    for i in range(EQ):
                        pv = pooled[:, :, bass.ds(q * EQ + i, 1)].rearrange("p b e -> p (b e)")
                        for hc in range(HC):
                            dst = bank[s][:, (i * HC + hc) * B:(i * HC + hc + 1) * B]
                            pe.matmul(dst, W1[s][:, i, hc * 128:(hc + 1) * 128], pv, start=True, stop=False)
                            ins = pe.matmul(dst, W1b[s][0:1, i, hc * 128:(hc + 1) * 128], ones[0:1, :], start=False, stop=True)
                    ins.then_inc(up_done[s], 1)
                    pe.wait_ge(gelu_done[s], kk + 1 + FREE)
                    pe.wait_ge(o_ready[s], kk + FREE)
                    for i in range(EQ):
                        dst = bank[2 + s][0:B, i * O:(i + 1) * O]
                        for hc in range(HC):
                            pe.matmul(dst, hT[s][:, i, hc, :], W2[s][:, i, hc, :], start=(hc == 0), stop=False)
                        ins = pe.matmul(dst, ones[0:1, :], W2b[s][0:1, i, :], start=False, stop=True)
                    ins.then_inc(down_done[s], 1)

            for s in range(2):
                pe.wait_ge(o_ready[s], E // EQ // 2 + FREE)
            with pe.Fori(0, B) as b:
                pe.wait_ge(ob_ready, b + 1)
                for j in range(NJ):
                    s = j % 2
                    pe.wait_ge(blk_loaded[s], (b * (NJ // 2) + j // 2 + 1) * 32)
                    for q in range(NQ):
                        h, c0 = q // 4, (q % 4) * 512
                        pe.wait_ge(ev[q], b * NJ + j + FREE)
                        pe.matmul(bank[q][:, :], Ob[0][h * E:(h + 1) * E, :], pin[s][h * E:(h + 1) * E, c0:c0 + 512],
                                  start=True, stop=False)
                        for t in range(4):
                            ins = pe.matmul(bank[q][:, t * 128:(t + 1) * 128], xin[s][:, h, (q % 4) * 4 + t, :], ident[:, :],
                                            is_transpose=True, start=False, stop=(t == 3))
                        ins.then_inc(blk_used[s] if q == NQ - 1 else sc_done, 1)


_INS = ['x', 'L0_conv_w', 'L0_ffn_gate_w', 'L0_ffn_gate_b', 'L0_ffn_weight1', 'L0_ffn_weight2']


def kernel(**inputs):
    import numpy as _np
    import concourse.bacc as _bacc
    from concourse import mybir as _mybir
    from concourse.bass_utils import run_bass_kernel_spmd as _run

    nc = _bacc.Bacc("TRN2", target_bir_lowering=False, num_devices=1)
    arrays, args = {}, []
    for name in _INS:
        a = _np.ascontiguousarray(inputs[name])
        if name == 'x':
            a = a.reshape(B, C, N)
        arrays[f"in_{name}_dram"] = a
        args.append(nc.dram_tensor(f"in_{name}_dram", a.shape, _mybir.dt.from_np(a.dtype), kind="ExternalInput").ap())
    o = nc.dram_tensor("out_0_dram", (B, C, N), _mybir.dt.float32, kind="ExternalOutput").ap()
    build(nc, *args, o)
    r = _run(nc, [arrays], core_ids=[0])
    return r.results[0]["out_0_dram"].reshape(B, C, 128, 128)
```

```python
import concourse.bass as bass
from concourse import mybir
from contextlib import ExitStack
from itertools import count

B, C, N = 16, 128, 128 * 128
E, H, O, K = 64, 512, 128, 8
HALF = N // 2
T = 128
IH = 4
GT = 2 * IH
NG = N // (GT * T)
NC = 2 * NG
XP = 8
XW = HALF // XP
TAIL = 8
HC = H // 128
EQ = 4
NW = 4
NK = E // (EQ * NW)
NJ = 4
JT = HALF // NJ
HIT = 200.0
DVE_STEPS = 13
LEAD = 4
FREE = 1
NQ = 8


def build(nc, x, conv_w, gate_w, gate_b, w1, w2, out):
    f32, bf16, u32 = mybir.dt.float32, mybir.dt.bfloat16, mybir.dt.uint32
    ALU, ACT, AX = mybir.AluOpType, mybir.ActivationFunctionType, mybir.AxisListType

    tok = nc.dram_tensor("tok_scratch", (B, 2, T, N // (2 * T), C), f32, kind="Internal").ap()
    prob = nc.dram_tensor("prob_scratch", (B, 128, HALF), f32, kind="Internal").ap()
    eout = nc.dram_tensor("eout_scratch", (B, E, O), f32, kind="Internal").ap()
    cur = nc.dram_tensor("cur_scratch", (2, T, N // (2 * T), C), f32, kind="Internal").ap()
    cur_rows = cur.rearrange("h p t c -> (h p t) c")

    ctx = ExitStack()
    with ctx:
        def sb(name, shape, dt=f32):
            return ctx.enter_context(nc.sbuf_tensor(name, shape, dt))

        def sem(name):
            return ctx.enter_context(nc.semaphore(name))

        bank = [ctx.enter_context(nc.psum_tensor(f"bank{i}", [128, 512], f32)) for i in range(8)]

        X = sb("X", [128, 2, HALF])
        Y = sb("Y", [128, 2, HALF // T, C])
        P = sb("P", [128, HALF + TAIL])
        hit = sb("hit", [128, HALF + TAIL], mybir.dt.uint8)
        ident = sb("ident", [128, 128])
        fold = sb("fold", [128, E])
        convT = sb("convT", [128, 128])
        gwT = sb("gwT", [128, E])
        gb = sb("gb", [128, 1])
        U0 = sb("U0", [E, C])
        pad = sb("pad", [1, 64])
        ones = sb("ones", [1, B])
        mhalf = sb("mhalf", [128, GT])
        quarter = sb("quarter", [128, GT])
        wsel = sb("wsel", [128, K])
        row0 = sb("row0", [128, 1])
        zT = sb("zT", [128, 2, GT, 128])
        x2 = sb("x2", [128, 2, 512])
        Ls = sb("Ls", [128, 2, IH, 2, E])
        st = sb("st", [128, 4, GT, 6])
        r1 = sb("r1", [128, NG * GT])
        nmr1 = sb("nmr1", [128, NG * GT])
        r2 = sb("r2", [128, 4, GT])
        gram = sb("gram", [128, 128])
        BT = sb("BT", [128, 128])
        pt = sb("pt", [128, 8, GT])
        cand = sb("cand", [128, NG * 8])
        top = sb("top", [128, 8])
        candm = sb("candm", [64, 16])
        e16 = sb("e16", [64, 16])
        rep16 = sb("rep16", [64, 16])
        selm = sb("selm", [64, 16])
        u8 = sb("u8", [64, 8])
        sel = sb("sel", [128, 8])
        negmax = sb("negmax", [128, 1])
        esum = sb("esum", [128, 1])
        es = sb("es", [64, 2])
        sinv = sb("sinv", [128, B])
        inv = sb("inv", [128, 1])
        idx = sb("idx", [128, 8], u32)
        ia = sb("ia", [128, 8], u32)
        ib = sb("ib", [128, 8], u32)
        rows = sb("rows", [128, 8], u32)
        G = sb("G", [128, K, 128])
        stg = sb("stg", [128, K, 6])
        rw = sb("rw", [128, K])
        nmrw = sb("nmrw", [128, K])
        U = sb("U", [128, K, 128])
        pooled = sb("pooled", [128, B, E])
        Xf = X[:, :, :].rearrange("p h n -> p (h n)")
        Yf = Y[:, :, :, :].rearrange("p h t c -> p (h t c)")
        Pf = P[:, 0:HALF]
        W1 = [Xf[:, s * 4096:s * 4096 + 2048].rearrange("p (e h) -> p e h", e=EQ) for s in range(NW)]
        W2 = [Xf[:, s * 4096 + 2048:s * 4096 + 4096].rearrange("p (e a o) -> p e a o", e=EQ, a=HC) for s in range(NW)]
        W1b = Yf[0:E, 8192:8192 + H]
        W2b = Yf[:, 8704:8704 + O]
        hT = [Yf[:, 9216 + s * 256:9472 + s * 256].rearrange("p (h e b) -> p h e b", e=EQ, h=HC) for s in range(2)]
        Osb = [Yf[0:B, 10240 + s * 512:10752 + s * 512] for s in range(NW)]
        O2 = Yf[:, 12288:14336].rearrange("p (b o) -> p b o", b=B)
        Ob = [Yf[:, 14336 + h * O:14336 + (h + 1) * O] for h in range(2)]
        xin = [Xf[:, s * 4096:(s + 1) * 4096].rearrange("p (h t c) -> p h t c", h=2, c=C) for s in range(NJ)]
        pin = [Yf[:, s * 2048:(s + 1) * 2048] for s in range(NJ)]
        osb = [Pf[:, s * 4096:(s + 1) * 4096].rearrange("p (h n) -> p h n", h=2) for s in range(2)]

        s_const = sem("s_const")
        s_ident = sem("s_ident")
        s_small = sem("s_small")
        s_gwc = sem("s_gwc")
        s_tr0 = sem("s_tr0")
        s_prep = sem("s_prep")
        x_loaded = [sem(f"x_loaded{j}") for j in range(XP)]
        xT_ready = sem("xT_ready")
        st1_ready = sem("st1_ready")
        norm1_ready = sem("norm1_ready")
        z_ready = sem("z_ready")
        gram_done = sem("gram_done")
        gram_copied = sem("gram_copied")
        bt_done = sem("bt_done")
        bt_copied = sem("bt_copied")
        y_ready = sem("y_ready")
        xT_copied = sem("xT_copied")
        x2T_ready = sem("x2T_ready")
        x2_tr = sem("x2_tr")
        x2_ready = sem("x2_ready")
        logit_done = sem("logit_done")
        st2_ready = sem("st2_ready")
        norm2_ready = sem("norm2_ready")
        ls_ready = sem("ls_ready")
        lT_done = sem("lT_done")
        l_ready = sem("l_ready")
        x2T_stored = [sem(f"x2T_stored{j}") for j in range(XP)]
        negmax_ready = sem("negmax_ready")
        exp_ready = sem("exp_ready")
        p_ready = sem("p_ready")
        p_stored = sem("p_stored")
        rows_ready = sem("rows_ready")
        gathered = sem("gathered")
        stg_ready = sem("stg_ready")
        normg_ready = sem("normg_ready")
        u_ready = sem("u_ready")
        pool_done = sem("pool_done")
        pooled_ready = sem("pooled_ready")
        dve_step = sem("dve_step")
        cand_done = sem("cand_done")
        u8_done = sem("u8_done")
        sel_done = sem("sel_done")
        before_step, after_step, gather_step = sem("before_step"), sem("after_step"), sem("gather_step")
        w_loaded = [sem(f"w_loaded{s}") for s in range(NW)]
        b_loaded = sem("b_loaded")
        up_done = [sem(f"up_done{s}") for s in range(NW)]
        gelu_done = [sem(f"gelu_done{s}") for s in range(NW)]
        down_done = [sem(f"down_done{s}") for s in range(NW)]
        o_ready = [sem(f"o_ready{s}") for s in range(NW)]
        o_stored = [sem(f"o_stored{s}") for s in range(NW)]
        o2_loaded = sem("o2_loaded")
        o2_ready = sem("o2_ready")
        ob_ready = sem("ob_ready")
        blk_loaded = [sem(f"blk_loaded{s}") for s in range(NJ)]
        blk_used = [sem(f"blk_used{s}") for s in range(NJ)]
        sc_done = sem("sc_done")
        ev = [sem(f"ev{q}") for q in range(NQ)]
        out_stored = [sem(f"out_stored{s}") for s in range(2)]


        block = ctx.enter_context(nc.Block())

        def xtile(k, h, i):
            return X[:, h, (k * IH + i) * T:(k * IH + i + 1) * T]

        start_free = [gram_done, lT_done, l_ready, logit_done, ls_ready, norm1_ready, norm2_ready, p_stored, pool_done, pooled_ready, x2T_ready, x2_ready, x2_tr, xT_copied, z_ready,
                      *x2T_stored, *down_done, *o_stored, *gelu_done, *o_ready, *ev, *blk_used, *out_stored]

        @block.sync
        def _(sp):
            for semaphore in start_free:
                sp.sem_inc(semaphore, FREE)
            sp.dma_start(gram[:, :], conv_w).then_inc(s_small, 16)
            sp.dma_start(BT[0:E, :], gate_w).then_inc(s_small, 16)
            for h in range(2):
                sp.dma_start(gb[h * E:(h + 1) * E, :], gate_b.rearrange("(e a) -> e a", a=1)).then_inc(s_small, 16)

            def load_x(b, j):
                src = x[b].rearrange("c (h n) -> c h n", h=2)
                sp.dma_start(X[:, :, j * XW:(j + 1) * XW], src[:, :, j * XW:(j + 1) * XW]).then_inc(x_loaded[j], 16)

            def load_w(q, s):
                sp.dma_start(W1[s], w1[bass.ds(q * EQ, EQ), 0:C, :].rearrange("e c h -> c e h")).then_inc(w_loaded[s], 16)
                sp.dma_start(W2[s].rearrange("p e a o -> p e (a o)"),
                             w2[bass.ds(q * EQ, EQ), 0:H, :].rearrange("e (p a) o -> p e (a o)", a=HC)).then_inc(w_loaded[s], 16)

            for j in range(XP):
                load_x(0, j)

            def image(b, more):
                for k in range(1, NG, 2):
                    j = k // 2
                    sp.wait_ge(x2T_ready, b * NC + 2 * k + 2 + FREE)
                    sp.dma_start(tok[b, :, :, (k - 1) * IH:(k + 1) * IH, :].rearrange("h p t c -> p h t c"),
                                 Y[:, :, (k - 1) * IH:(k + 1) * IH, :]).then_inc(x2T_stored[j], 16)
                    sp.dma_start(cur[:, :, (k - 1) * IH:(k + 1) * IH, :].rearrange("h p t c -> p h t c"),
                                 Y[:, :, (k - 1) * IH:(k + 1) * IH, :]).then_inc(x2T_stored[j], 16)
                    if more:
                        sp.wait_ge(y_ready, b * NC + 2 * k + 2)
                        load_x(b + 1, j)

            def store_prob(b):
                sp.wait_ge(p_ready, b + 1)
                sp.dma_start(prob[b], P[:, 0:HALF]).then_inc(p_stored, 16)

            with sp.Fori(0, B - 1) as b:
                image(b, True)
                store_prob(b)
            image(B - 1, False)
            sp.wait_ge(y_ready, B * NC)
            for s in range(NW):
                load_w(s, s)
            for j in range(XP):
                sp.wait_ge(x2T_stored[j], 32 * B + FREE)
            sp.dma_start(W1b, w1[:, C, :]).then_inc(b_loaded, 16)
            for h in range(2):
                sp.dma_start(W2b[h * E:(h + 1) * E, :], w2[:, H, :]).then_inc(b_loaded, 16)
            store_prob(B - 1)

            def store_o(kk, s):
                sp.wait_ge(o_ready[s], kk + 1 + FREE)
                sp.dma_start(eout[:, bass.ds((kk * NW + s) * EQ, EQ), :],
                             Osb[s].rearrange("b (e o) -> b e o", o=O)).then_inc(o_stored[s], 16)

            with sp.Fori(0, NK - 1) as kk:
                for s in range(NW):
                    sp.wait_ge(down_done[s], kk + 1 + FREE)
                    load_w(kk * NW + NW + s, s)
                    store_o(kk, s)
            for s in range(NW):
                store_o(NK - 1, s)
            for s in range(NW):
                sp.wait_ge(o_stored[s], 16 * NK + FREE)
            for h in range(2):
                sp.dma_start(O2[h * E:(h + 1) * E], eout.rearrange("b e o -> e b o")).then_inc(o2_loaded, 16)

            sp.wait_ge(p_stored, 16 * B + FREE)
            for j in range(XP):
                sp.wait_ge(x2T_stored[j], 32 * B + FREE)
            with sp.Fori(0, B) as b:
                for j in range(NJ):
                    s = j
                    sp.wait_ge(blk_used[s], b + FREE)
                    sp.dma_start(xin[s], tok[b, :, :, j * (JT // T):(j + 1) * (JT // T), :].rearrange("h p t c -> p h t c")
                                 ).then_inc(blk_loaded[s], 16)
                    sp.dma_start(pin[s], prob[b, :, j * JT:(j + 1) * JT]).then_inc(blk_loaded[s], 16)

        @block.gpsimd
        def _(pool):
            pool.memset(ident[:, :], 0.0).then_inc(s_ident, 1)
            pool.memset(fold[:, :], 0.0).then_inc(s_ident, 1)
            pool.wait_ge(s_ident, 2)
            pool.affine_select(out=ident[:, :], in_=ident[:, :], compare_op=ALU.not_equal, fill=1.0, base=0,
                               pattern=[[-1, 128]], channel_multiplier=1).then_inc(s_ident, 1)
            pool.affine_select(out=fold[:, :], in_=fold[:, :], compare_op=ALU.not_equal, fill=1.0, base=0,
                               pattern=[[-1, E]], channel_multiplier=1).then_inc(s_ident, 1)
            pool.wait_ge(s_ident, 4)
            pool.affine_select(out=fold[:, :], in_=fold[:, :], compare_op=ALU.not_equal, fill=1.0, base=-E,
                               pattern=[[-1, E]], channel_multiplier=1).then_inc(s_const, 1)
            pool.memset(mhalf[:, :], -0.5)
            pool.memset(quarter[:, :], 0.25).then_inc(s_const, 1)
            pool.memset(P[:, HALF:HALF + TAIL], 0.0).then_inc(s_const, 1)
            pool.memset(row0[:, :], float(HALF)).then_inc(s_const, 1)
            pool.memset(ones[:, :], 1.0).then_inc(s_const, 1)
            pool.wait_ge(s_const, 5)
            pool.memset(row0[0:E, :], 0.0).then_inc(s_const, 1)
            pool.wait_ge(s_const, 6)

            def rsqrt(src, r, eps, step, done):
                w = src.shape[1]
                diff, sq, both, part, total, nmean, v = (pt[:, i, 0:w] for i in range(7))
                pool.tensor_tensor(diff, src[:, :, 1], src[:, :, 4], ALU.subtract)
                pool.tensor_tensor(total, src[:, :, 1], src[:, :, 4], ALU.add)
                pool.tensor_tensor(both, src[:, :, 2], src[:, :, 5], ALU.add).then_inc(step, 1)
                pool.wait_ge(step, done + 1)
                pool.tensor_tensor(sq, diff, diff, ALU.mult)
                pool.tensor_scalar(nmean, total, -0.5, None, ALU.mult)
                pool.tensor_scalar(part, both, 1.0 / C, eps, ALU.mult, ALU.add).then_inc(step, 1)
                pool.wait_ge(step, done + 2)
                pool.tensor_tensor(sq, sq, quarter[:, 0:w], ALU.mult).then_inc(step, 1)
                pool.wait_ge(step, done + 3)
                pool.tensor_tensor(v, sq, part, ALU.add).then_inc(step, 1)
                pool.wait_ge(step, done + 4)
                return pool.tensor_tensor(r, v, mhalf[:, 0:w], ALU.pow)

            def norm_before(i, k):
                pool.wait_ge(st1_ready, i * NG + (k + 1))
                r = r1[:, k * GT:(k + 1) * GT]
                rsqrt(st[:, k % 4], r, 1e-6, before_step, i * (NG * 5) + k * 5).then_inc(before_step, 1)
                pool.wait_ge(before_step, i * (NG * 5) + (k * 5 + 5))
                pool.tensor_tensor(nmr1[:, k * GT:(k + 1) * GT], pt[:, 5, 0:GT], r, ALU.mult).then_inc(norm1_ready, 1)

            def norms_after(b):
                for k in range(NG):
                    pool.wait_ge(st2_ready, b * NG + (k + 1))
                    pool.wait_ge(ls_ready, b * NG + max(k - 3, 0) + FREE)
                    rsqrt(st[:, k % 4], r2[:, k % 4], 1e-5, after_step, b * (NG * 4) + k * 4).then_inc(norm2_ready, 1)

            def gather(k):
                pool.indirect_dma_start(out=G[:, k, :], out_offset=None, in_=cur_rows[:, :],
                                        in_offset=bass.IndirectOffsetOnAxis(ap=rows[:, k:k + 1], axis=0)
                                        ).then_inc(gathered, 16)

            def gather_first(b, imgs, stored):
                for j in range(XP):
                    pool.wait_ge(x2T_stored[j], stored)
                pool.wait_ge(rows_ready, imgs)
                pool.tensor_tensor(pt[:, 7, 0:1], mhalf[:, 0:1], mhalf[:, 0:1], ALU.add)

            def weigh(b):
                pool.wait_ge(stg_ready, b + 1)
                rsqrt(stg[:, :, :], pt[:, 7, 0:K], 1e-5, gather_step, b * 6).then_inc(gather_step, 1)
                pool.wait_ge(gather_step, b * 6 + 5)
                pool.tensor_tensor(rw[:, :], pt[:, 7, 0:K], wsel[:, :], ALU.mult).then_inc(gather_step, 1)
                pool.wait_ge(gather_step, b * 6 + 6)
                pool.tensor_tensor(nmrw[:, :], rw[:, :], pt[:, 5, 0:K], ALU.mult).then_inc(normg_ready, 1)

            def choose(b, more):
                imgs = pool.snap(b + 1)
                stored = pool.snap(b * 32 + 32 + FREE)
                if more:
                    pool.wait_ge(x2T_ready, b * NC + NC + FREE)
                for k in range(NG):
                    if more:
                        norm_before(b + 1, k)
                    if k == 6:
                        gather_first(b, imgs, stored)
                    if 6 <= k < 10:
                        gather(2 * (k - 6))
                        gather(2 * (k - 6) + 1)
                    if k == 13:
                        weigh(b)

            for k in range(NG):
                norm_before(0, k)
            with pool.Fori(0, B - 1) as b:
                norms_after(b)
                choose(b, True)
            norms_after(B - 1)
            choose(B - 1, False)

        @block.scalar
        def _(act):
            def copy_xT(i, k, earlier=True):
                act.wait_ge(xT_ready, i * NG + (k + 1))
                if earlier and k % 2 == 0:
                    act.wait_ge(x2T_stored[k // 2], i * 32 + FREE)
                for h in range(2):
                    ins = act.activation(Y[:, h, k * IH:(k + 1) * IH, :].rearrange("p t c -> p (t c)"),
                                         bank[2 * (k % 3) + h][:, :], ACT.Copy)
                ins.then_inc(xT_copied, 1)

            def norm_z(i, k):
                act.wait_ge(norm1_ready, i * NG + (k + 1) + FREE)
                act.wait_ge(gram_done, i * NG + max(k - 1, 0) + FREE)
                for t in range(GT):
                    h, c = t // IH, k * GT + t
                    ins = act.activation(zT[:, k % 2, t, :], Y[:, h, k * IH + t % IH, :],
                                         ACT.Identity, bias=nmr1[:, c:c + 1], scale=r1[:, c:c + 1])
                ins.then_inc(z_ready, 1)

            def matrices(i):
                act.wait_ge(gram_done, i * NG + NG + FREE)
                act.activation(gram[:, :], bank[6][:, 0:128], ACT.Copy, scale=1.0 / N).then_inc(gram_copied, 1)
                act.wait_ge(bt_done, i + 1)
                act.activation(BT[:, :], bank[7][:, 0:128], ACT.Copy).then_inc(bt_copied, 1)

            def after(b):
                def copy_x2(g):
                    act.wait_ge(x2_tr, b * NC + (g + 1) + FREE)
                    act.wait_ge(logit_done, b * NC + max(g - 1, 0) + FREE)
                    act.activation(x2[:, g % 2, :], bank[3 + g % 2][:, :], ACT.Copy).then_inc(x2_ready, 1)

                def scale_l(k):
                    act.wait_ge(logit_done, b * NC + (2 * k + 2) + FREE)
                    act.wait_ge(norm2_ready, b * NG + (k + 1) + FREE)
                    act.wait_ge(lT_done, b * NG + max(k - 1, 0) + FREE)
                    for t in range(GT):
                        ins = act.activation(Ls[:, k % 2, t % IH, t // IH, :], bank[5 + k % 2][:, t * E:(t + 1) * E],
                                             ACT.Copy, scale=r2[:, k % 4, t:t + 1])
                    ins.then_inc(ls_ready, 1)

                def copy_l(k):
                    act.wait_ge(lT_done, b * NG + (k + 1) + FREE)
                    if k == 0:
                        act.wait_ge(p_stored, b * 16 + FREE)
                    act.activation(P[:, k * 512:(k + 1) * 512], bank[7][:, :], ACT.Identity,
                                   bias=gb[:, 0:1]).then_inc(l_ready, 1)

                for g in range(NC + 6):
                    if g < NC:
                        copy_x2(g)
                    if g % 2 == 1 and 0 <= (g - 3) // 2 < NG and g >= 3:
                        scale_l((g - 3) // 2)
                    if g % 2 == 0 and 0 <= (g - 6) // 2 < NG and g >= 6:
                        copy_l((g - 6) // 2)

            def choose(b, more):
                if more:
                    for k in range(LEAD):
                        copy_xT(b + 1, k)
                act.wait_ge(negmax_ready, b + 1)
                act.activation(e16[:, :], candm[:, :], ACT.Exp, bias=negmax[0:64, 0:1])
                act.activation(P[:, 0:HALF], P[:, 0:HALF], ACT.Exp, bias=negmax[:, 0:1],
                               accum_out=esum[:, 0:1]).then_inc(exp_ready, 1)
                for k in range(NG):
                    if more:
                        if k + LEAD < NG:
                            copy_xT(b + 1, k + LEAD)
                        norm_z(b + 1, k)
                    if k == 14:
                        act.wait_ge(normg_ready, b + 1)
                        act.wait_ge(pool_done, b + FREE)
                        for i in range(K):
                            ins = act.activation(U[:, i, :], G[:, i, :], ACT.Identity, bias=nmrw[:, i:i + 1],
                                                 scale=rw[:, i:i + 1])
                        ins.then_inc(u_ready, 1)
                if more:
                    matrices(b + 1)

            act.wait_ge(s_small, 64)
            act.wait_ge(s_const, 6)
            for k in range(LEAD):
                copy_xT(0, k, earlier=False)
            for k in range(NG):
                if k + LEAD < NG:
                    copy_xT(0, k + LEAD, earlier=False)
                norm_z(0, k)
            matrices(0)
            with act.Fori(0, B - 1) as b:
                after(b)
                choose(b, True)
            after(B - 1)
            choose(B - 1, False)

            for j in range(XP):
                act.wait_ge(x2T_stored[j], B * 32 + FREE)
            with act.Fori(0, NK) as kk:
                for s in range(NW):
                    act.wait_ge(up_done[s], kk + 1)
                    act.wait_ge(down_done[(s + 2) % NW], kk + (s >= 2) + FREE)
                    act.activation(hT[s % 2].rearrange("p h e b -> p (h e b)"), bank[s % 2][:, 0:EQ * HC * B],
                                   ACT.Gelu).then_inc(gelu_done[s], 1)

            act.wait_ge(p_stored, B * 16 + FREE)
            with act.Fori(0, B) as b:
                for j in range(NJ):
                    s = j % 2
                    act.wait_ge(out_stored[s], (b * (NJ // 2) + j // 2) * 16 + FREE)
                    for q in range(0, NQ, 2):
                        act.wait_ge(sc_done, (b * NJ + j) * (NQ - 1) + (q + 1))
                        act.activation(osb[s][:, q // 4, (q % 4) * 512:(q % 4 + 1) * 512], bank[q][:, :],
                                       ACT.Copy).then_inc(ev[q], 1)
                    for q in range(NQ):
                        act.wait_ge(ev[q], b * NJ + (j + 1) + FREE)
                    act.dma_start(out[b].rearrange("c (h n) -> c h n", h=2)[:, :, j * JT:(j + 1) * JT],
                                  osb[s]).then_inc(out_stored[s], 16)
            for s in range(2):
                act.wait_ge(out_stored[s], B * (NJ // 2) * 16 + FREE)

        @block.vector
        def _(dve):
            dve.wait_ge(s_small, 64)
            dve.bn_stats(st[0:E, 0, 0, :], BT[0:E, :]).then_inc(s_gwc, 1)
            dve.wait_ge(s_gwc, 1)
            dve.bn_aggr(top[0:E, 0:2], st[0:E, 0, 0, :]).then_inc(s_gwc, 1)
            dve.wait_ge(s_gwc, 2)
            dve.tensor_scalar(U0[:, :], BT[0:E, :], top[0:E, 0:1], None, ALU.subtract).then_inc(s_gwc, 1)
            dve.wait_ge(s_tr0, 1)
            dve.tensor_copy(convT[:, :], bank[0][:, 0:128]).then_inc(s_prep, 1)
            dve.tensor_copy(gwT[:, :], bank[0][:, 128:128 + E]).then_inc(s_prep, 1)

            def carry():
                cell = next(cells) % 64
                dve.memset(pad[:, cell:cell + 1], 0.0)

            cells = count()

            def stats_before(i, k):
                dve.wait_ge(xT_copied, i * NG + (k + 1) + FREE)
                if k >= 4:
                    dve.wait_ge(norm1_ready, i * NG + (k - 3) + FREE)
                for t in range(GT):
                    ins = dve.bn_stats(st[:, k % 4, t, :], Y[:, t // IH, k * IH + t % IH, :])
                ins.then_inc(st1_ready, 1)

            def after(b):
                def tokens(g):
                    k, cc = g // 2, g % 2
                    dve.wait_ge(y_ready, b * NC + (g + 1))
                    for t in range(4):
                        h, i = t // 2, 2 * cc + t % 2
                        c = k * GT + h * IH + i
                        tile = Y[:, h, k * IH + i, :]
                        ins = dve.scalar_tensor_tensor(tile, bank[g % 3][:, t * 128:(t + 1) * 128], r1[:, c:c + 1], tile,
                                                       ALU.mult, ALU.add)
                    ins.then_inc(x2T_ready, 1)

                def stats(g):
                    k, cc = g // 2, g % 2
                    dve.wait_ge(x2T_ready, b * NC + (g + 1) + FREE)
                    if cc == 0 and k >= 4:
                        dve.wait_ge(norm2_ready, b * NG + (k - 3) + FREE)
                    for t in range(4):
                        h, i = t // 2, 2 * cc + t % 2
                        ins = dve.bn_stats(st[:, k % 4, h * IH + i, :], Y[:, h, k * IH + i, :])
                    if cc == 1:
                        ins.then_inc(st2_ready, 1)

                def best(k):
                    dve.wait_ge(l_ready, b * NG + (k + 1) + FREE)
                    carry()
                    return dve.max(cand[:, k * 8:(k + 1) * 8], P[:, k * 512:(k + 1) * 512])

                dve.wait_ge(norm1_ready, b * NG + NG + FREE)
                for g in range(NC + 1):
                    if g < NC:
                        tokens(g)
                    if g >= 1:
                        stats(g - 1)
                    if g % 2 == 0 and g >= 10:
                        best((g - 10) // 2)
                for k in range(NG - 4, NG):
                    ins = best(k)
                return ins

            def choose(b, more, last_best):
                n = [0]

                def step(ins):
                    n[0] += 1
                    ins.then_inc(dve_step, 1)
                    dve.wait_ge(dve_step, b * DVE_STEPS + n[0])

                def settled(ins, semaphore):
                    ins.then_inc(semaphore, 1)
                    dve.wait_ge(semaphore, b + 1)
                    carry()

                settled(last_best, cand_done)
                step(dve.max(top[:, :], cand[:, :]))
                dve.tensor_copy(candm[:, 8:16], top[64:128, :])
                step(dve.tensor_copy(candm[:, 0:8], top[0:64, :]))
                step(dve.tensor_scalar(negmax[0:64, :], candm[:, 0:1], candm[:, 8:9], -1.0, ALU.max, ALU.mult))
                dve.tensor_copy(negmax[64:128, :], negmax[0:64, :]).then_inc(negmax_ready, 1)
                for k in range(NG):
                    if more:
                        stats_before(b + 1, k)
                    if k == LEAD - 1:
                        dve.wait_ge(exp_ready, b + 1)
                        carry()
                        settled(dve.max(u8[:, :], e16[:, :]), u8_done)
                        step(dve.match_replace(rep16[:, :], u8[:, :], e16[:, :], 0.0))
                        step(dve.tensor_tensor(selm[:, :], e16[:, :], rep16[:, :], ALU.subtract))
                        dve.tensor_copy(sel[64:128, :], selm[:, 8:16])
                        step(dve.tensor_copy(sel[0:64, :], selm[:, 0:8]))
                        step(dve.tensor_copy(es[:, 0:1], esum[64:128, :]))
                        step(dve.tensor_tensor(es[:, 1:2], es[:, 0:1], esum[0:64, :], ALU.add))
                        step(dve.reciprocal(inv[0:64, :], es[:, 1:2]))
                        step(dve.tensor_copy(inv[64:128, :], inv[0:64, :]))
                        dve.tensor_scalar(wsel[:, :], sel[:, :], inv[:, 0:1], None, ALU.mult)
                        settled(dve.tensor_copy(sinv[:, bass.ds(b, 1)], inv[:, :]), sel_done)
                        step(dve.max_index(idx[:, :], sel[:, :], P[:, :]))
                        dve.tensor_scalar(ia[:, :], idx[:, :], T - 1, 6, ALU.bitwise_and, ALU.logical_shift_left)
                        step(dve.tensor_scalar(ib[:, :], idx[:, :], 7, None, ALU.logical_shift_right))
                        dve.scalar_tensor_tensor(rows[:, :], ia[:, :], row0[:, 0:1], ib[:, :], ALU.add,
                                                 ALU.add).then_inc(rows_ready, 1)
                    if k == 6:
                        step(dve.match_replace(hit[:, :], sel[:, :], P[:, :], HIT))
                    if k == 8:
                        dve.scalar_tensor_tensor(P[:, :], hit[:, :], HIT / 2, P[:, :], ALU.is_gt, ALU.mult).then_inc(p_ready, 1)
                    if k == 13:
                        dve.wait_ge(gathered, b * (16 * K) + 16 * K)
                        for i in range(K):
                            ins = dve.bn_stats(stg[:, i, :], G[:, i, :])
                        ins.then_inc(stg_ready, 1)
                dve.wait_ge(pool_done, b + 1 + FREE)
                dve.tensor_copy(pooled[:, bass.ds(b, 1), :].rearrange("p a e -> p (a e)"), bank[4][:, 0:E]
                                ).then_inc(pooled_ready, 1)
                assert n[0] == DVE_STEPS

            dve.wait_ge(s_const, 6)
            for k in range(NG):
                stats_before(0, k)
            with dve.Fori(0, B - 1) as b:
                choose(b, True, after(b))
            choose(B - 1, False, after(B - 1))

            with dve.Fori(0, NK) as kk:
                for s in range(NW):
                    dve.wait_ge(down_done[s], kk + 1 + FREE)
                    dve.wait_ge(o_stored[s], kk * 16 + FREE)
                    dve.tensor_copy(Osb[s], bank[2 + s % 2][0:B, :]).then_inc(o_ready[s], 1)
            dve.memset(Ob[0][E:128, :], 0.0)
            dve.memset(Ob[1][0:E, :], 0.0)
            dve.wait_ge(b_loaded, 48)
            dve.wait_ge(o2_loaded, 32)
            dve.tensor_tensor(O2, O2, W2b.unsqueeze(1).to_broadcast([128, B, O]), ALU.add).then_inc(o2_ready, 1)
            dve.wait_ge(o2_ready, 1)
            dve.tensor_tensor(O2, O2, sinv[:, :].unsqueeze(2).to_broadcast([128, B, O]), ALU.mult).then_inc(o2_ready, 1)
            dve.wait_ge(o2_ready, 2)
            with dve.Fori(0, B) as b:
                dve.wait_ge(blk_used[NJ - 1], b + FREE)
                for h in range(2):
                    rows_h = slice(h * E, (h + 1) * E)
                    ins = dve.tensor_copy(Ob[h][rows_h, :], O2[rows_h, bass.ds(b, 1), :].rearrange("p a o -> p (a o)"))
                ins.then_inc(ob_ready, 1)
                for j in range(NJ):
                    s = j % 2
                    dve.wait_ge(out_stored[s], (b * (NJ // 2) + j // 2) * 16 + FREE)
                    for q in range(1, NQ, 2):
                        if q == NQ - 1:
                            dve.wait_ge(blk_used[j], b + 1 + FREE)
                        else:
                            dve.wait_ge(sc_done, (b * NJ + j) * (NQ - 1) + (q + 1))
                        dve.tensor_copy(osb[s][:, q // 4, (q % 4) * 512:(q % 4 + 1) * 512], bank[q][:, :]).then_inc(ev[q], 1)

        @block.tensor
        def _(pe):
            pe.wait_ge(s_const, 6)
            pe.wait_ge(s_gwc, 3)
            pe.wait_ge(s_small, 64)
            pe.transpose(bank[0][:, 0:128], gram[:, :], ident[:, :])
            pe.transpose(bank[0][:, 128:128 + E], U0[:, :], ident[0:E, 0:E]).then_inc(s_tr0, 1)
            pe.wait_ge(s_prep, 2)

            def xT_tiles(i, k):
                if k % 2 == 0:
                    pe.wait_ge(x_loaded[k // 2], i * 16 + 16)
                if k >= 3:
                    pe.wait_ge(xT_copied, i * NG + (k - 2) + FREE)
                for t in range(GT):
                    ins = pe.transpose(bank[2 * (k % 3) + t // IH][:, (t % IH) * 128:(t % IH + 1) * 128],
                                       xtile(k, t // IH, t % IH), ident[:, :])
                ins.then_inc(xT_ready, 1)

            def gram_tiles(i, k):
                pe.wait_ge(z_ready, i * NG + (k + 1) + FREE)
                for t in range(GT):
                    z = zT[:, k % 2, t, :]
                    ins = pe.matmul(bank[6][:, 0:128], z, z, start=(k == 0 and t == 0), stop=(k == NG - 1 and t == GT - 1))
                ins.then_inc(gram_done, 1)

            def before(i):
                for k in range(NG + LEAD + 1):
                    if k < NG:
                        xT_tiles(i, k)
                    if k > LEAD:
                        gram_tiles(i, k - LEAD - 1)

            def matrices(i):
                pe.wait_ge(gram_copied, i + 1)
                pe.matmul(bank[7][:, 0:128], gram[:, :], convT[:, :], start=True, stop=True).then_inc(bt_done, 1)
                pe.wait_ge(bt_copied, i + 1)

            def pool_rows(b):
                pe.wait_ge(u_ready, b + 1)
                for i in range(K):
                    ins = pe.matmul(bank[4][:, 0:E], U[:, i, :], fold[:, :], start=(i == 0), stop=(i == K - 1))
                ins.then_inc(pool_done, 1)

            def after(b):
                def conv(g):
                    k, cc = g // 2, g % 2
                    if g >= 3:
                        pe.wait_ge(x2T_ready, b * NC + (g - 2) + FREE)
                    for t in range(4):
                        ins = pe.matmul(bank[g % 3][:, t * 128:(t + 1) * 128], xtile(k, t // 2, 2 * cc + t % 2), BT[:, :],
                                        start=True, stop=True)
                    ins.then_inc(y_ready, 1)

                def x2_back(g):
                    k, cc = g // 2, g % 2
                    pe.wait_ge(x2T_ready, b * NC + (g + 1) + FREE)
                    if g >= 2:
                        pe.wait_ge(x2_ready, b * NC + (g - 1) + FREE)
                    if g == 1:
                        pe.wait_ge(pooled_ready, b + FREE)
                    for t in range(4):
                        ins = pe.transpose(bank[3 + g % 2][:, t * 128:(t + 1) * 128],
                                           Y[:, t // 2, k * IH + 2 * cc + t % 2, :], ident[:, :])
                    ins.then_inc(x2_tr, 1)

                def logits(g):
                    k, cc = g // 2, g % 2
                    pe.wait_ge(x2_ready, b * NC + (g + 1) + FREE)
                    if cc == 0:
                        pe.wait_ge(ls_ready, b * NG + max(k - 1, 0) + FREE)
                    for t in range(4):
                        c = (t // 2) * IH + 2 * cc + t % 2
                        ins = pe.matmul(bank[5 + k % 2][:, c * E:(c + 1) * E], x2[:, g % 2, t * 128:(t + 1) * 128], gwT[:, :],
                                        start=True, stop=True)
                    ins.then_inc(logit_done, 1)

                def logits_T(k):
                    pe.wait_ge(ls_ready, b * NG + (k + 1) + FREE)
                    pe.wait_ge(l_ready, b * NG + k + FREE)
                    for i in range(IH):
                        ins = pe.transpose(bank[7][:, i * 128:(i + 1) * 128], Ls[:, k % 2, i].rearrange("p h e -> p (h e)"), ident[:, :])
                    ins.then_inc(lT_done, 1)

                for g in range(NC + 6):
                    if g < NC:
                        conv(g)
                    if 1 <= g <= NC:
                        x2_back(g - 1)
                    if 2 <= g <= NC + 1:
                        logits(g - 2)
                    if g % 2 == 0 and g >= 6 and (g - 6) // 2 < NG:
                        logits_T((g - 6) // 2)
                pe.wait_ge(x2_ready, b * NC + NC + FREE)
                pe.wait_ge(ls_ready, b * NG + NG + FREE)
                pe.wait_ge(l_ready, b * NG + NG + FREE)

            before(0)
            matrices(0)
            with pe.Fori(0, B - 1) as b:
                after(b)
                before(b + 1)
                pool_rows(b)
                matrices(b + 1)
            after(B - 1)
            pool_rows(B - 1)

            pe.wait_ge(pooled_ready, B + FREE)
            pe.wait_ge(b_loaded, 48)

            def up(kk, s):
                q = kk * NW + s
                pe.wait_ge(w_loaded[s], kk * 32 + 32)
                pe.wait_ge(gelu_done[(s + 2) % NW], kk + (s >= 2) + FREE)
                for hc in range(HC):
                    dst = bank[s % 2][:, hc * EQ * B:(hc + 1) * EQ * B]
                    pe.matmul(dst.rearrange("p (e b) -> p e b", e=EQ), W1b[:, hc::HC],
                              ident[0:E, bass.ds(q * EQ, EQ)].unsqueeze(2).to_broadcast([E, EQ, B]), start=True, stop=False)
                    for i in range(EQ):
                        pv = pooled[:, :, bass.ds(q * EQ + i, 1)].rearrange("p b e -> p (b e)")
                        ins = pe.matmul(dst[:, i * B:(i + 1) * B], W1[s][:, i, hc::HC], pv, start=False, stop=(i == EQ - 1))
                ins.then_inc(up_done[s], 1)

            def down(kk, s):
                pe.wait_ge(gelu_done[s], kk + 1 + FREE)
                pe.wait_ge(o_ready[(s + 2) % NW], kk + (s >= 2) + FREE)
                for i in range(EQ):
                    dst = bank[2 + s % 2][0:B, i * O:(i + 1) * O]
                    for hc in range(HC):
                        ins = pe.matmul(dst, hT[s % 2][:, hc, i, :], W2[s][:, i, hc, :], start=(hc == 0), stop=(hc == HC - 1))
                ins.then_inc(down_done[s], 1)

            up(0, 0)
            with pe.Fori(0, NK - 1) as kk:
                for s in range(NW):
                    up(kk + (s + 1) // NW, (s + 1) % NW)
                    down(kk, s)
            for s in range(NW):
                if s < NW - 1:
                    up(NK - 1, s + 1)
                down(NK - 1, s)

            for s in range(NW):
                pe.wait_ge(o_ready[s], NK + FREE)
            with pe.Fori(0, B) as b:
                pe.wait_ge(ob_ready, b + 1)
                for j in range(NJ):
                    pe.wait_ge(blk_loaded[j], b * 32 + 32)
                    for q in range(NQ):
                        h, c0 = q // 4, (q % 4) * 512
                        pe.wait_ge(ev[q], b * NJ + j + FREE)
                        pe.matmul(bank[q][:, :], Ob[h], pin[j][:, c0:c0 + 512], start=True, stop=False)
                        for t in range(4):
                            ins = pe.matmul(bank[q][:, t * 128:(t + 1) * 128], xin[j][:, h, (q % 4) * 4 + t, :], ident[:, :],
                                            is_transpose=True, start=False, stop=(t == 3))
                        ins.then_inc(blk_used[j] if q == NQ - 1 else sc_done, 1)


_INS = ['x', 'L0_conv_w', 'L0_ffn_gate_w', 'L0_ffn_gate_b', 'L0_ffn_weight1', 'L0_ffn_weight2']


def kernel(**inputs):
    import numpy as _np
    import concourse.bacc as _bacc
    from concourse import mybir as _mybir
    from concourse.bass_utils import run_bass_kernel_spmd as _run

    nc = _bacc.Bacc("TRN2", target_bir_lowering=False, num_devices=1)
    arrays, args = {}, []
    for name in _INS:
        a = _np.ascontiguousarray(inputs[name])
        if name == 'x':
            a = a.reshape(B, C, N)
        arrays[f"in_{name}_dram"] = a
        args.append(nc.dram_tensor(f"in_{name}_dram", a.shape, _mybir.dt.from_np(a.dtype), kind="ExternalInput").ap())
    o = nc.dram_tensor("out_0_dram", (B, C, N), _mybir.dt.float32, kind="ExternalOutput").ap()
    build(nc, *args, o)
    r = _run(nc, [arrays], core_ids=[0])
    return r.results[0]["out_0_dram"].reshape(B, C, 128, 128)
```

```python
import concourse.bass as bass
from concourse import mybir
from contextlib import ExitStack
from itertools import count

B, C, N = 16, 128, 128 * 128
E, H, O, K = 64, 512, 128, 8
HALF = N // 2
T = 128
IH = 4
GT = 2 * IH
NG = N // (GT * T)
NC = 2 * NG
XP = 8
XW = HALF // XP
TAIL = 8
HC = H // 128
EQ = 4
NW = 4
NK = E // (EQ * NW)
NJ = 4
JT = HALF // NJ
HIT = 200.0
DVE_STEPS = 13
LEAD = 5
ZS = 3
EARLY = 2
FREE = 1
NQ = 8


def build(nc, x, conv_w, gate_w, gate_b, w1, w2, out):
    f32, u32 = mybir.dt.float32, mybir.dt.uint32
    ALU, ACT = mybir.AluOpType, mybir.ActivationFunctionType

    tok = nc.dram_tensor("tok_scratch", (B, 2, T, N // (2 * T), C), f32, kind="Internal").ap()
    prob = nc.dram_tensor("prob_scratch", (B, 128, HALF), f32, kind="Internal").ap()
    eout = nc.dram_tensor("eout_scratch", (B, E, O), f32, kind="Internal").ap()
    cur = nc.dram_tensor("cur_scratch", (2, T, N // (2 * T), C), f32, kind="Internal").ap()
    cur_rows = cur.rearrange("h p t c -> (h p t) c")

    ctx = ExitStack()
    with ctx:
        def sb(name, shape, dt=f32):
            return ctx.enter_context(nc.sbuf_tensor(name, shape, dt))

        def sem(name):
            return ctx.enter_context(nc.semaphore(name))

        bank = [ctx.enter_context(nc.psum_tensor(f"bank{i}", [128, 512], f32)) for i in range(8)]

        X = sb("X", [128, 2, HALF])
        Y = sb("Y", [128, 2, HALF // T, C])
        P = sb("P", [128, HALF + TAIL])
        hit = sb("hit", [128, HALF + TAIL], mybir.dt.uint8)
        ident = sb("ident", [128, 128])
        fold = sb("fold", [128, E])
        convT = sb("convT", [128, 128])
        gwT = sb("gwT", [128, E])
        gb = sb("gb", [128, 1])
        U0 = sb("U0", [E, C])
        pad = sb("pad", [1, 16])
        rv1 = sb("rv1", [128, 8, GT])
        rv2 = sb("rv2", [128, 4, GT])
        rvg = sb("rvg", [128, K])
        wsel = sb("wsel", [128, K])
        row0 = sb("row0", [128, 1])
        zT = sb("zT", [128, ZS, GT, 128])
        x2 = sb("x2", [128, 2, 512])
        Ls = sb("Ls", [128, 2, IH, 2, E])
        st = sb("st", [128, 4, GT, 6])
        r1 = sb("r1", [128, NG * GT])
        nm1 = sb("nm1", [128, NG * GT])
        nmr1 = sb("nmr1", [128, NG * GT])
        r2 = sb("r2", [128, 4, GT])
        gram = sb("gram", [128, 128])
        BT = sb("BT", [128, 128])
        pt = sb("pt", [128, 8, GT])
        cand = sb("cand", [128, NG * 8])
        top = sb("top", [128, 8])
        candm = sb("candm", [64, 16])
        e16 = sb("e16", [64, 16])
        rep16 = sb("rep16", [64, 16])
        selm = sb("selm", [64, 16])
        u8 = sb("u8", [64, 8])
        sel = sb("sel", [128, 8])
        negmax = sb("negmax", [128, 1])
        esum = sb("esum", [128, 1])
        es = sb("es", [64, 2])
        sinv = sb("sinv", [128, B])
        inv = sb("inv", [128, 1])
        idx = sb("idx", [128, 8], u32)
        ia = sb("ia", [128, 8], u32)
        ib = sb("ib", [128, 8], u32)
        rows = sb("rows", [128, 8], u32)
        G = sb("G", [128, K, 128])
        stg = sb("stg", [128, K, 6])
        rg = sb("rg", [128, K])
        nmg = sb("nmg", [128, K])
        rw = sb("rw", [128, K])
        nmrw = sb("nmrw", [128, K])
        U = sb("U", [128, K, 128])
        pooled = sb("pooled", [128, B, E])
        Xf = X[:, :, :].rearrange("p h n -> p (h n)")
        Yf = Y[:, :, :, :].rearrange("p h t c -> p (h t c)")
        Pf = P[:, 0:HALF]
        W1 = [Xf[:, s * 4096:s * 4096 + 2048].rearrange("p (e h) -> p e h", e=EQ) for s in range(NW)]
        W2 = [Xf[:, s * 4096 + 2048:s * 4096 + 4096].rearrange("p (e a o) -> p e a o", e=EQ, a=HC) for s in range(NW)]
        W1b = Yf[0:E, 8192:8192 + H]
        W2b = Yf[:, 8704:8704 + O]
        hT = [Yf[:, 9216 + s * 256:9472 + s * 256].rearrange("p (h e b) -> p h e b", e=EQ, h=HC) for s in range(2)]
        Osb = [Yf[0:B, 10240 + s * 512:10752 + s * 512] for s in range(NW)]
        O2 = Yf[:, 12288:14336].rearrange("p (b o) -> p b o", b=B)
        Ob = [Yf[:, 14336 + h * O:14336 + (h + 1) * O] for h in range(2)]
        xin = [Xf[:, s * 4096:(s + 1) * 4096].rearrange("p (h t c) -> p h t c", h=2, c=C) for s in range(NJ)]
        pin = [Yf[:, s * 2048:(s + 1) * 2048] for s in range(NJ)]
        osb = [Pf[:, s * 4096:(s + 1) * 4096].rearrange("p (h n) -> p h n", h=2) for s in range(2)]

        s_const = sem("s_const")
        s_ident = sem("s_ident")
        s_small = sem("s_small")
        s_gwc = sem("s_gwc")
        s_tr0 = sem("s_tr0")
        s_prep = sem("s_prep")
        x_loaded = [sem(f"x_loaded{j}") for j in range(XP)]
        xT_ready = sem("xT_ready")
        st1_ready = sem("st1_ready")
        v1_ready = sem("v1_ready")
        rv1_ready = sem("rv1_ready")
        r1_ready = sem("r1_ready")
        nmr1_ready = sem("nmr1_ready")
        z_ready = sem("z_ready")
        zd_ready = sem("zd_ready")
        gram_done = sem("gram_done")
        gram_copied = sem("gram_copied")
        bt_done = sem("bt_done")
        bt_copied = sem("bt_copied")
        y_ready = sem("y_ready")
        xT_copied = sem("xT_copied")
        x2T_ready = sem("x2T_ready")
        x2_tr = sem("x2_tr")
        x2_ready = sem("x2_ready")
        logit_done = sem("logit_done")
        st2_ready = sem("st2_ready")
        v2_ready = sem("v2_ready")
        rv2_ready = sem("rv2_ready")
        r2_ready = sem("r2_ready")
        ls_ready = sem("ls_ready")
        lT_done = sem("lT_done")
        l_ready = sem("l_ready")
        x2T_stored = [sem(f"x2T_stored{j}") for j in range(XP)]
        negmax_ready = sem("negmax_ready")
        exp_ready = sem("exp_ready")
        p_ready = sem("p_ready")
        p_stored = sem("p_stored")
        rows_ready = sem("rows_ready")
        gathered = sem("gathered")
        stg_ready = sem("stg_ready")
        vg_ready = sem("vg_ready")
        rvg_ready = sem("rvg_ready")
        rg_ready = sem("rg_ready")
        normg_ready = sem("normg_ready")
        u_ready = sem("u_ready")
        pool_done = sem("pool_done")
        pooled_ready = sem("pooled_ready")
        dve_step = sem("dve_step")
        cand_done = sem("cand_done")
        u8_done = sem("u8_done")
        sel_done = sem("sel_done")
        before_step, after_step, gather_step = sem("before_step"), sem("after_step"), sem("gather_step")
        w_loaded = [sem(f"w_loaded{s}") for s in range(NW)]
        b_loaded = sem("b_loaded")
        up_done = [sem(f"up_done{s}") for s in range(NW)]
        gelu_done = [sem(f"gelu_done{s}") for s in range(NW)]
        down_done = [sem(f"down_done{s}") for s in range(NW)]
        o_ready = [sem(f"o_ready{s}") for s in range(NW)]
        o_stored = [sem(f"o_stored{s}") for s in range(NW)]
        o2_loaded = sem("o2_loaded")
        o2_ready = sem("o2_ready")
        ob_ready = sem("ob_ready")
        blk_loaded = [sem(f"blk_loaded{s}") for s in range(NJ)]
        blk_used = [sem(f"blk_used{s}") for s in range(NJ)]
        sc_done = sem("sc_done")
        ev = [sem(f"ev{q}") for q in range(NQ)]
        out_stored = [sem(f"out_stored{s}") for s in range(2)]


        block = ctx.enter_context(nc.Block())

        def xtile(k, h, i):
            return X[:, h, (k * IH + i) * T:(k * IH + i + 1) * T]

        def vector_tiles(k):
            return (3, 7) if k < 12 else (1, 3, 5, 7)

        start_free = [gram_done, lT_done, l_ready, logit_done, ls_ready, v1_ready, v2_ready, p_stored, pool_done,
                      pooled_ready, x2T_ready, x2_ready, x2_tr, xT_copied, z_ready,
                      *x2T_stored, *down_done, *o_stored, *gelu_done, *o_ready, *ev, *blk_used, *out_stored]

        @block.sync
        def _(sp):
            for semaphore in start_free:
                sp.sem_inc(semaphore, FREE)
            sp.dma_start(gram[:, :], conv_w).then_inc(s_small, 16)
            sp.dma_start(BT[0:E, :], gate_w).then_inc(s_small, 16)
            for h in range(2):
                sp.dma_start(gb[h * E:(h + 1) * E, :], gate_b.rearrange("(e a) -> e a", a=1)).then_inc(s_small, 16)

            def load_x(b, j):
                src = x[b].rearrange("c (h n) -> c h n", h=2)
                sp.dma_start(X[:, :, j * XW:(j + 1) * XW], src[:, :, j * XW:(j + 1) * XW]).then_inc(x_loaded[j], 16)

            def load_w(q, s):
                sp.dma_start(W1[s], w1[bass.ds(q * EQ, EQ), 0:C, :].rearrange("e c h -> c e h")).then_inc(w_loaded[s], 16)
                sp.dma_start(W2[s].rearrange("p e a o -> p e (a o)"),
                             w2[bass.ds(q * EQ, EQ), 0:H, :].rearrange("e (p a) o -> p e (a o)", a=HC)).then_inc(w_loaded[s], 16)

            for j in range(XP):
                load_x(0, j)

            def image(b, more):
                for k in range(1, NG, 2):
                    j = k // 2
                    sp.wait_ge(x2T_ready, b * NC + 2 * k + 2 + FREE)
                    sp.dma_start(tok[b, :, :, (k - 1) * IH:(k + 1) * IH, :].rearrange("h p t c -> p h t c"),
                                 Y[:, :, (k - 1) * IH:(k + 1) * IH, :]).then_inc(x2T_stored[j], 16)
                    sp.dma_start(cur[:, :, (k - 1) * IH:(k + 1) * IH, :].rearrange("h p t c -> p h t c"),
                                 Y[:, :, (k - 1) * IH:(k + 1) * IH, :]).then_inc(x2T_stored[j], 16)
                    if more:
                        sp.wait_ge(y_ready, b * NC + 2 * k + 2)
                        load_x(b + 1, j)

            def store_prob(b):
                sp.wait_ge(p_ready, b + 1)
                sp.dma_start(prob[b], P[:, 0:HALF]).then_inc(p_stored, 16)

            with sp.Fori(0, B - 1) as b:
                image(b, True)
                store_prob(b)
            image(B - 1, False)
            sp.wait_ge(y_ready, B * NC)
            for s in range(NW):
                load_w(s, s)
            for j in range(XP):
                sp.wait_ge(x2T_stored[j], 32 * B + FREE)
            sp.dma_start(W1b, w1[:, C, :]).then_inc(b_loaded, 16)
            for h in range(2):
                sp.dma_start(W2b[h * E:(h + 1) * E, :], w2[:, H, :]).then_inc(b_loaded, 16)
            store_prob(B - 1)

            def store_o(kk, s):
                sp.wait_ge(o_ready[s], kk + 1 + FREE)
                sp.dma_start(eout[:, bass.ds((kk * NW + s) * EQ, EQ), :],
                             Osb[s].rearrange("b (e o) -> b e o", o=O)).then_inc(o_stored[s], 16)

            with sp.Fori(0, NK - 1) as kk:
                for s in range(NW):
                    sp.wait_ge(down_done[s], kk + 1 + FREE)
                    load_w(kk * NW + NW + s, s)
                    store_o(kk, s)
            def load_tokens(b, j):
                sp.dma_start(xin[j], tok[b, :, :, j * (JT // T):(j + 1) * (JT // T), :].rearrange("h p t c -> p h t c")
                             ).then_inc(blk_loaded[j], 16)

            def load_prob(b, j):
                sp.dma_start(pin[j], prob[b, :, j * JT:(j + 1) * JT]).then_inc(blk_loaded[j], 16)

            for s in range(NW):
                store_o(NK - 1, s)
                if s < NW - 1:
                    load_tokens(0, s)
            for s in range(NW):
                sp.wait_ge(o_stored[s], 16 * NK + FREE)
            for h in range(2):
                sp.dma_start(O2[h * E:(h + 1) * E], eout.rearrange("b e o -> e b o")).then_inc(o2_loaded, 16)

            load_tokens(0, NJ - 1)
            sp.wait_ge(p_stored, 16 * B + FREE)
            for j in range(NJ):
                load_prob(0, j)
            with sp.Fori(1, B) as b:
                for j in range(NJ):
                    sp.wait_ge(blk_used[j], b + FREE)
                    load_tokens(b, j)
                    load_prob(b, j)

        @block.gpsimd
        def _(pool):
            pool.memset(ident[:, :], 0.0).then_inc(s_ident, 1)
            pool.memset(fold[:, :], 0.0).then_inc(s_ident, 1)
            pool.wait_ge(s_ident, 2)
            pool.affine_select(out=ident[:, :], in_=ident[:, :], compare_op=ALU.not_equal, fill=1.0, base=0,
                               pattern=[[-1, 128]], channel_multiplier=1).then_inc(s_ident, 1)
            pool.affine_select(out=fold[:, :], in_=fold[:, :], compare_op=ALU.not_equal, fill=1.0, base=0,
                               pattern=[[-1, E]], channel_multiplier=1).then_inc(s_ident, 1)
            pool.wait_ge(s_ident, 4)
            pool.affine_select(out=fold[:, :], in_=fold[:, :], compare_op=ALU.not_equal, fill=1.0, base=-E,
                               pattern=[[-1, E]], channel_multiplier=1).then_inc(s_const, 1)
            pool.memset(pt[:, 7, :], 1.0).then_inc(s_const, 1)
            pool.memset(P[:, HALF:HALF + TAIL], 0.0).then_inc(s_const, 1)
            pool.memset(row0[:, :], float(HALF)).then_inc(s_const, 1)
            pool.wait_ge(s_const, 4)
            pool.memset(row0[0:E, :], 0.0).then_inc(s_const, 1)
            pool.wait_ge(s_const, 5)

            def variance(src, v, nmean, eps, step, done):
                w = src.shape[1]
                diff, sq, both, part, total = (pt[:, i, 0:w] for i in range(5))
                pool.tensor_tensor(diff, src[:, :, 1], src[:, :, 4], ALU.subtract)
                pool.tensor_tensor(total, src[:, :, 1], src[:, :, 4], ALU.add)
                pool.tensor_tensor(both, src[:, :, 2], src[:, :, 5], ALU.add).then_inc(step, 1)
                pool.wait_ge(step, done + 1)
                pool.tensor_tensor(sq, diff, diff, ALU.mult)
                pool.tensor_scalar(nmean, total, -0.5, None, ALU.mult)
                pool.tensor_scalar(part, both, 4.0 / C, 4.0 * eps, ALU.mult, ALU.add).then_inc(step, 1)
                pool.wait_ge(step, done + 2)
                return pool.tensor_tensor(v, sq, part, ALU.add)

            def norm_before(i, k):
                pool.wait_ge(st1_ready, i * NG + (k + 1))
                variance(st[:, k % 4], rv1[:, k % 8], nm1[:, k * GT:(k + 1) * GT], 1e-6, before_step,
                        i * (NG * 2) + k * 2).then_inc(v1_ready, 1)

            def shift_before(i, k):
                pool.wait_ge(r1_ready, i * NG + (k + 1))
                pool.tensor_tensor(nmr1[:, k * GT:(k + 1) * GT], nm1[:, k * GT:(k + 1) * GT],
                                   r1[:, k * GT:(k + 1) * GT], ALU.mult).then_inc(nmr1_ready, 1)

            def norms_after(b):
                for k in range(NG):
                    pool.wait_ge(st2_ready, b * NG + (k + 1))
                    pool.wait_ge(ls_ready, b * NG + max(k - 3, 0) + FREE)
                    variance(st[:, k % 4], rv2[:, k % 4], pt[:, 5, :], 1e-5, after_step,
                            b * (NG * 2) + k * 2).then_inc(v2_ready, 1)

            def gather(k):
                pool.indirect_dma_start(out=G[:, k, :], out_offset=None, in_=cur_rows[:, :],
                                        in_offset=bass.IndirectOffsetOnAxis(ap=rows[:, k:k + 1], axis=0)
                                        ).then_inc(gathered, 16)

            def gather_first(b, imgs, stored):
                for j in range(XP):
                    pool.wait_ge(x2T_stored[j], stored)
                pool.wait_ge(rows_ready, imgs)
                pool.tensor_tensor(pt[:, 6, 0:1], pt[:, 7, 0:1], pt[:, 7, 0:1], ALU.add)

            def norm_gathered(b):
                pool.wait_ge(stg_ready, b + 1)
                variance(stg[:, :, :], rvg[:, :], nmg[:, :], 1e-5, gather_step, b * 3).then_inc(vg_ready, 1)

            def weigh(b):
                pool.wait_ge(rg_ready, b + 1)
                pool.tensor_tensor(rw[:, :], rg[:, :], wsel[:, :], ALU.mult).then_inc(gather_step, 1)
                pool.wait_ge(gather_step, b * 3 + 3)
                pool.tensor_tensor(nmrw[:, :], rw[:, :], nmg[:, :], ALU.mult).then_inc(normg_ready, 1)

            def choose(b, more):
                imgs = pool.snap(b + 1)
                stored = pool.snap(b * 32 + 32 + FREE)
                if more:
                    pool.wait_ge(x2T_ready, b * NC + NC + FREE)
                for k in range(NG):
                    if more:
                        if k >= LEAD:
                            for j in range(0 if k == LEAD else k - 1, k):
                                shift_before(b + 1, j)
                        norm_before(b + 1, k)
                    if k == 5:
                        gather_first(b, imgs, stored)
                    if 5 <= k < 9:
                        gather(2 * (k - 5))
                        gather(2 * (k - 5) + 1)
                    if k == 13:
                        norm_gathered(b)
                    if k == 15:
                        weigh(b)
                if more:
                    shift_before(b + 1, NG - 1)

            for k in range(NG):
                norm_before(0, k)
                if k >= 1:
                    shift_before(0, k - 1)
            shift_before(0, NG - 1)
            with pool.Fori(0, B - 1) as b:
                norms_after(b)
                choose(b, True)
            norms_after(B - 1)
            choose(B - 1, False)

        @block.scalar
        def _(act):
            def copy_xT(i, k, earlier=True):
                act.wait_ge(xT_ready, i * NG + (k + 1))
                if earlier and k % 2 == 0:
                    act.wait_ge(x2T_stored[k // 2], i * 32 + FREE)
                for h in range(2):
                    ins = act.activation(Y[:, h, k * IH:(k + 1) * IH, :].rearrange("p t c -> p (t c)"),
                                         bank[2 * (k % 3) + h][:, :], ACT.Copy)
                ins.then_inc(xT_copied, 1)

            def root_before(i, k):
                act.wait_ge(rv1_ready, i * NG + (k + 1))
                act.activation(r1[:, k * GT:(k + 1) * GT], rv1[:, k % 8, :], ACT.Sqrt, scale=4.0).then_inc(r1_ready, 1)

            def norm_z(i, k):
                act.wait_ge(nmr1_ready, i * NG + (k + 1))
                act.wait_ge(gram_done, i * NG + max(k - ZS + 1, 0) + FREE)
                for t in range(GT):
                    if t in vector_tiles(k):
                        continue
                    h, c = t // IH, k * GT + t
                    ins = act.activation(zT[:, k % ZS, t, :], Y[:, h, k * IH + t % IH, :],
                                         ACT.Identity, bias=nmr1[:, c:c + 1], scale=r1[:, c:c + 1])
                ins.then_inc(z_ready, 1)

            def group_before(i, k, earlier=True):
                if k == 0:
                    for j in range(ZS):
                        root_before(i, j)
                if k + LEAD < NG:
                    copy_xT(i, k + LEAD, earlier)
                if ZS <= k + 1 < NG:
                    root_before(i, k + 1)
                norm_z(i, k)

            def matrices(i):
                act.wait_ge(gram_done, i * NG + NG + FREE)
                act.activation(gram[:, :], bank[6][:, 0:128], ACT.Copy, scale=1.0 / N).then_inc(gram_copied, 1)
                act.wait_ge(bt_done, i + 1)
                act.activation(BT[:, :], bank[7][:, 0:128], ACT.Copy).then_inc(bt_copied, 1)

            def after(b, more):
                def copy_x2(g):
                    act.wait_ge(x2_tr, b * NC + (g + 1) + FREE)
                    act.wait_ge(logit_done, b * NC + max(g - 1, 0) + FREE)
                    act.activation(x2[:, g % 2, :], bank[3 + g % 2][:, :], ACT.Copy).then_inc(x2_ready, 1)

                def scale_l(k):
                    act.wait_ge(rv2_ready, b * NG + (k + 1))
                    act.activation(r2[:, k % 4, :], rv2[:, k % 4, :], ACT.Sqrt, scale=4.0).then_inc(r2_ready, 1)
                    act.wait_ge(r2_ready, b * NG + (k + 1))
                    act.wait_ge(logit_done, b * NC + (2 * k + 2) + FREE)
                    act.wait_ge(lT_done, b * NG + max(k - 1, 0) + FREE)
                    for t in range(GT):
                        ins = act.activation(Ls[:, k % 2, t % IH, t // IH, :], bank[5 + k % 2][:, t * E:(t + 1) * E],
                                             ACT.Copy, scale=r2[:, k % 4, t:t + 1])
                    ins.then_inc(ls_ready, 1)

                def copy_l(k):
                    act.wait_ge(lT_done, b * NG + (k + 1) + FREE)
                    if k == 0:
                        act.wait_ge(p_stored, b * 16 + FREE)
                    act.activation(P[:, k * 512:(k + 1) * 512], bank[7][:, :], ACT.Identity,
                                   bias=gb[:, 0:1]).then_inc(l_ready, 1)

                for g in range(NC + 6):
                    if g < NC:
                        copy_x2(g)
                    if g % 2 == 1 and 0 <= (g - 3) // 2 < NG and g >= 3:
                        scale_l((g - 3) // 2)
                    if g % 2 == 0 and 0 <= (g - 6) // 2 < NG and g >= 6:
                        copy_l((g - 6) // 2)
                    if g == NC + 3 and more:
                        for k in range(EARLY):
                            copy_xT(b + 1, k)

            def choose(b, more):
                if more:
                    for k in range(EARLY, LEAD):
                        copy_xT(b + 1, k)
                act.wait_ge(negmax_ready, b + 1)
                act.activation(e16[:, :], candm[:, :], ACT.Exp, bias=negmax[0:64, 0:1])
                act.activation(P[:, 0:HALF], P[:, 0:HALF], ACT.Exp, bias=negmax[:, 0:1],
                               accum_out=esum[:, 0:1]).then_inc(exp_ready, 1)
                for k in range(NG):
                    if more:
                        group_before(b + 1, k)
                    if k == 14:
                        act.wait_ge(rvg_ready, b + 1)
                        act.activation(rg[:, :], rvg[:, :], ACT.Sqrt, scale=4.0).then_inc(rg_ready, 1)
                if more:
                    matrices(b + 1)

            act.wait_ge(s_small, 64)
            act.wait_ge(s_const, 5)
            for k in range(LEAD):
                copy_xT(0, k, earlier=False)
            for k in range(NG):
                group_before(0, k, earlier=False)
            matrices(0)
            with act.Fori(0, B - 1) as b:
                after(b, True)
                choose(b, True)
            after(B - 1, False)
            choose(B - 1, False)

            for j in range(XP):
                act.wait_ge(x2T_stored[j], B * 32 + FREE)
            with act.Fori(0, NK) as kk:
                for s in range(NW):
                    act.wait_ge(up_done[s], kk + 1)
                    act.wait_ge(down_done[(s + 2) % NW], kk + (s >= 2) + FREE)
                    act.activation(hT[s % 2].rearrange("p h e b -> p (h e b)"), bank[s % 2][:, 0:EQ * HC * B],
                                   ACT.Gelu).then_inc(gelu_done[s], 1)

            act.wait_ge(p_stored, B * 16 + FREE)
            with act.Fori(0, B) as b:
                for j in range(NJ):
                    s = j % 2
                    act.wait_ge(out_stored[s], (b * (NJ // 2) + j // 2) * 16 + FREE)
                    for q in range(0, NQ, 2):
                        act.wait_ge(sc_done, (b * NJ + j) * (NQ - 1) + (q + 1))
                        act.activation(osb[s][:, q // 4, (q % 4) * 512:(q % 4 + 1) * 512], bank[q][:, :],
                                       ACT.Copy).then_inc(ev[q], 1)
                    for q in range(NQ):
                        act.wait_ge(ev[q], b * NJ + (j + 1) + FREE)
                    act.dma_start(out[b].rearrange("c (h n) -> c h n", h=2)[:, :, j * JT:(j + 1) * JT],
                                  osb[s]).then_inc(out_stored[s], 16)
            for s in range(2):
                act.wait_ge(out_stored[s], B * (NJ // 2) * 16 + FREE)

        @block.vector
        def _(dve):
            dve.wait_ge(s_small, 64)
            dve.bn_stats(st[0:E, 0, 0, :], BT[0:E, :]).then_inc(s_gwc, 1)
            dve.wait_ge(s_gwc, 1)
            dve.bn_aggr(top[0:E, 0:2], st[0:E, 0, 0, :]).then_inc(s_gwc, 1)
            dve.wait_ge(s_gwc, 2)
            dve.tensor_scalar(U0[:, :], BT[0:E, :], top[0:E, 0:1], None, ALU.subtract).then_inc(s_gwc, 1)
            dve.wait_ge(s_tr0, 1)
            dve.tensor_copy(convT[:, :], bank[0][:, 0:128]).then_inc(s_prep, 1)
            dve.tensor_copy(gwT[:, :], bank[0][:, 128:128 + E]).then_inc(s_prep, 1)

            def carry():
                cell = next(cells) % 16
                dve.memset(pad[:, cell:cell + 1], 0.0)

            cells = count()

            def stats_before(i, k, earlier=True):
                dve.wait_ge(xT_copied, i * NG + (k + 1) + FREE)
                if k >= 4:
                    dve.wait_ge(v1_ready, i * NG + (k - 3) + FREE)
                elif earlier:
                    dve.wait_ge(v2_ready, i * NG + (k - 3) + FREE)
                for t in range(GT):
                    ins = dve.bn_stats(st[:, k % 4, t, :], Y[:, t // IH, k * IH + t % IH, :])
                ins.then_inc(st1_ready, 1)

            def inverse_before(i, k):
                dve.wait_ge(v1_ready, i * NG + (k + 1) + FREE)
                dve.reciprocal(rv1[:, k % 8, :], rv1[:, k % 8, :]).then_inc(rv1_ready, 1)

            def norm_z(i, k):
                dve.wait_ge(r1_ready, i * NG + (k + 1))
                dve.wait_ge(gram_done, i * NG + max(k - ZS + 1, 0) + FREE)
                for t in vector_tiles(k):
                    h, c = t // IH, k * GT + t
                    ins = dve.tensor_scalar(zT[:, k % ZS, t, :], Y[:, h, k * IH + t % IH, :], nm1[:, c:c + 1],
                                            r1[:, c:c + 1], ALU.add, ALU.mult)
                ins.then_inc(zd_ready, 1)

            def tokens(b, g):
                k, cc = g // 2, g % 2
                if g == 0:
                    dve.wait_ge(r1_ready, b * NG + NG)
                dve.wait_ge(y_ready, b * NC + (g + 1))
                for t in range(4):
                    h, i = t // 2, 2 * cc + t % 2
                    c = k * GT + h * IH + i
                    tile = Y[:, h, k * IH + i, :]
                    ins = dve.scalar_tensor_tensor(tile, bank[g % 3][:, t * 128:(t + 1) * 128], r1[:, c:c + 1], tile,
                                                   ALU.mult, ALU.add)
                ins.then_inc(x2T_ready, 1)

            def after(b, more):
                def stats(g):
                    k, cc = g // 2, g % 2
                    dve.wait_ge(x2T_ready, b * NC + (g + 1) + FREE)
                    if cc == 0 and k >= 4:
                        dve.wait_ge(v2_ready, b * NG + (k - 3) + FREE)
                    for t in range(4):
                        h, i = t // 2, 2 * cc + t % 2
                        ins = dve.bn_stats(st[:, k % 4, h * IH + i, :], Y[:, h, k * IH + i, :])
                    if cc == 1:
                        ins.then_inc(st2_ready, 1)

                def inverse(k):
                    dve.wait_ge(v2_ready, b * NG + (k + 1) + FREE)
                    dve.reciprocal(rv2[:, k % 4, :], rv2[:, k % 4, :]).then_inc(rv2_ready, 1)

                def best(k):
                    dve.wait_ge(l_ready, b * NG + (k + 1) + FREE)
                    carry()
                    return dve.max(cand[:, k * 8:(k + 1) * 8], P[:, k * 512:(k + 1) * 512])

                for g in range(1, NC + 1):
                    if g < NC:
                        tokens(b, g)
                    if g >= 1:
                        stats(g - 1)
                    if g % 2 == 1 and g >= 3:
                        inverse((g - 3) // 2)
                    if g % 2 == 0 and g >= 10:
                        best((g - 10) // 2)
                for k in range(NG - 4, NG):
                    if k == NG - 3:
                        inverse(NG - 1)
                    ins = best(k)
                return ins

            def choose(b, more, last_best):
                n = [0]

                def step(ins):
                    n[0] += 1
                    ins.then_inc(dve_step, 1)
                    dve.wait_ge(dve_step, b * DVE_STEPS + n[0])

                def settled(ins, semaphore):
                    ins.then_inc(semaphore, 1)
                    dve.wait_ge(semaphore, b + 1)
                    carry()

                settled(last_best, cand_done)
                step(dve.max(top[:, :], cand[:, :]))
                dve.tensor_copy(candm[:, 8:16], top[64:128, :])
                step(dve.tensor_copy(candm[:, 0:8], top[0:64, :]))
                step(dve.tensor_scalar(negmax[0:64, :], candm[:, 0:1], candm[:, 8:9], -1.0, ALU.max, ALU.mult))
                dve.tensor_copy(negmax[64:128, :], negmax[0:64, :]).then_inc(negmax_ready, 1)
                for k in range(NG + 2):
                    if more:
                        if k < NG:
                            stats_before(b + 1, k)
                        if 1 <= k <= NG and k != LEAD:
                            inverse_before(b + 1, k - 1)
                        if k == LEAD - 1:
                            inverse_before(b + 1, k)
                        if k >= LEAD:
                            norm_z(b + 1, k - 2)
                    if k == LEAD - 1:
                        dve.wait_ge(exp_ready, b + 1)
                        carry()
                        settled(dve.max(u8[:, :], e16[:, :]), u8_done)
                        step(dve.match_replace(rep16[:, :], u8[:, :], e16[:, :], 0.0))
                        step(dve.tensor_tensor(selm[:, :], e16[:, :], rep16[:, :], ALU.subtract))
                        dve.tensor_copy(sel[64:128, :], selm[:, 8:16])
                        step(dve.tensor_copy(sel[0:64, :], selm[:, 0:8]))
                        step(dve.tensor_copy(es[:, 0:1], esum[64:128, :]))
                        step(dve.tensor_tensor(es[:, 1:2], es[:, 0:1], esum[0:64, :], ALU.add))
                        step(dve.reciprocal(inv[0:64, :], es[:, 1:2]))
                        step(dve.tensor_copy(inv[64:128, :], inv[0:64, :]))
                        dve.tensor_scalar(wsel[:, :], sel[:, :], inv[:, 0:1], None, ALU.mult)
                        if more:
                            for early in range(ZS):
                                norm_z(b + 1, early)
                        settled(dve.tensor_copy(sinv[:, bass.ds(b, 1)], inv[:, :]), sel_done)
                        step(dve.max_index(idx[:, :], sel[:, :], P[:, :]))
                        dve.tensor_scalar(ia[:, :], idx[:, :], T - 1, 6, ALU.bitwise_and, ALU.logical_shift_left)
                        step(dve.tensor_scalar(ib[:, :], idx[:, :], 7, None, ALU.logical_shift_right))
                        dve.scalar_tensor_tensor(rows[:, :], ia[:, :], row0[:, 0:1], ib[:, :], ALU.add,
                                                 ALU.add).then_inc(rows_ready, 1)
                    if k == 7:
                        step(dve.match_replace(hit[:, :], sel[:, :], P[:, :], HIT))
                    if 9 <= k < 13:
                        part = slice((k - 9) * (HALF // 4), (k - 8) * (HALF // 4))
                        ins = dve.scalar_tensor_tensor(P[:, part], hit[:, part], HIT / 2, P[:, part], ALU.is_gt, ALU.mult)
                        if k == 12:
                            ins.then_inc(p_ready, 1)
                    if k == (13 if more else 8):
                        dve.wait_ge(gathered, b * (16 * K) + 16 * K)
                        for i in range(K):
                            ins = dve.bn_stats(stg[:, i, :], G[:, i, :])
                        ins.then_inc(stg_ready, 1)
                    if k == (14 if more else 9):
                        dve.wait_ge(vg_ready, b + 1)
                        dve.reciprocal(rvg[:, :], rvg[:, :]).then_inc(rvg_ready, 1)
                dve.wait_ge(normg_ready, b + 1)
                dve.wait_ge(pool_done, b + FREE)
                for i in range(K):
                    ins = dve.tensor_scalar(U[:, i, :], G[:, i, :], rw[:, i:i + 1], nmrw[:, i:i + 1], ALU.mult, ALU.add)
                ins.then_inc(u_ready, 1)
                if more:
                    tokens(b + 1, 0)
                dve.wait_ge(pool_done, b + 1 + FREE)
                dve.tensor_copy(pooled[:, bass.ds(b, 1), :].rearrange("p a e -> p (a e)"), bank[4][:, 0:E]
                                ).then_inc(pooled_ready, 1)
                assert n[0] == DVE_STEPS

            dve.wait_ge(s_const, 5)
            for k in range(NG + 2):
                if k < NG:
                    stats_before(0, k, earlier=False)
                if 1 <= k <= NG:
                    inverse_before(0, k - 1)
                if k >= 2:
                    norm_z(0, k - 2)
            tokens(0, 0)
            with dve.Fori(0, B - 1) as b:
                choose(b, True, after(b, True))
            choose(B - 1, False, after(B - 1, False))

            with dve.Fori(0, NK) as kk:
                for s in range(NW):
                    dve.wait_ge(down_done[s], kk + 1 + FREE)
                    dve.wait_ge(o_stored[s], kk * 16 + FREE)
                    dve.tensor_copy(Osb[s], bank[2 + s % 2][0:B, :]).then_inc(o_ready[s], 1)
            dve.memset(Ob[0][E:128, :], 0.0)
            dve.memset(Ob[1][0:E, :], 0.0)
            dve.wait_ge(b_loaded, 48)
            dve.wait_ge(o2_loaded, 32)
            dve.tensor_tensor(O2, O2, W2b.unsqueeze(1).to_broadcast([128, B, O]), ALU.add).then_inc(o2_ready, 1)
            dve.wait_ge(o2_ready, 1)
            dve.tensor_tensor(O2, O2, sinv[:, :].unsqueeze(2).to_broadcast([128, B, O]), ALU.mult).then_inc(o2_ready, 1)
            dve.wait_ge(o2_ready, 2)
            with dve.Fori(0, B) as b:
                dve.wait_ge(blk_used[NJ - 1], b + FREE)
                for h in range(2):
                    rows_h = slice(h * E, (h + 1) * E)
                    ins = dve.tensor_copy(Ob[h][rows_h, :], O2[rows_h, bass.ds(b, 1), :].rearrange("p a o -> p (a o)"))
                ins.then_inc(ob_ready, 1)
                for j in range(NJ):
                    s = j % 2
                    dve.wait_ge(out_stored[s], (b * (NJ // 2) + j // 2) * 16 + FREE)
                    for q in range(1, NQ, 2):
                        if q == NQ - 1:
                            dve.wait_ge(blk_used[j], b + 1 + FREE)
                        else:
                            dve.wait_ge(sc_done, (b * NJ + j) * (NQ - 1) + (q + 1))
                        dve.tensor_copy(osb[s][:, q // 4, (q % 4) * 512:(q % 4 + 1) * 512], bank[q][:, :]).then_inc(ev[q], 1)

        @block.tensor
        def _(pe):
            pe.wait_ge(s_const, 5)
            pe.wait_ge(s_gwc, 3)
            pe.wait_ge(s_small, 64)
            pe.transpose(bank[0][:, 0:128], gram[:, :], ident[:, :])
            pe.transpose(bank[0][:, 128:128 + E], U0[:, :], ident[0:E, 0:E]).then_inc(s_tr0, 1)
            pe.wait_ge(s_prep, 2)

            def xT_tiles(i, k):
                if k % 2 == 0:
                    pe.wait_ge(x_loaded[k // 2], i * 16 + 16)
                if k >= 3:
                    pe.wait_ge(xT_copied, i * NG + (k - 2) + FREE)
                for t in range(GT):
                    ins = pe.transpose(bank[2 * (k % 3) + t // IH][:, (t % IH) * 128:(t % IH + 1) * 128],
                                       xtile(k, t // IH, t % IH), ident[:, :])
                ins.then_inc(xT_ready, 1)

            def gram_tiles(i, k):
                pe.wait_ge(z_ready, i * NG + (k + 1) + FREE)
                pe.wait_ge(zd_ready, i * NG + (k + 1))
                for t in range(GT):
                    z = zT[:, k % ZS, t, :]
                    ins = pe.matmul(bank[6][:, 0:128], z, z, start=(k == 0 and t == 0), stop=(k == NG - 1 and t == GT - 1))
                ins.then_inc(gram_done, 1)

            def before(i, first):
                for k in range(first, NG + LEAD + 1):
                    if k < NG:
                        xT_tiles(i, k)
                    if k > LEAD:
                        gram_tiles(i, k - LEAD - 1)

            def matrix(i):
                pe.wait_ge(gram_copied, i + 1)
                pe.matmul(bank[7][:, 0:128], gram[:, :], convT[:, :], start=True, stop=True).then_inc(bt_done, 1)

            def pool_rows(b):
                pe.wait_ge(u_ready, b + 1)
                for i in range(K):
                    ins = pe.matmul(bank[4][:, 0:E], U[:, i, :], fold[:, :], start=(i == 0), stop=(i == K - 1))
                ins.then_inc(pool_done, 1)

            def conv(b, g):
                k, cc = g // 2, g % 2
                if g == 0:
                    pe.wait_ge(bt_copied, b + 1)
                if g >= 3:
                    pe.wait_ge(x2T_ready, b * NC + (g - 2) + FREE)
                for t in range(4):
                    ins = pe.matmul(bank[g % 3][:, t * 128:(t + 1) * 128], xtile(k, t // 2, 2 * cc + t % 2), BT[:, :],
                                    start=True, stop=True)
                ins.then_inc(y_ready, 1)

            def after(b, more):
                def x2_back(g):
                    k, cc = g // 2, g % 2
                    pe.wait_ge(x2T_ready, b * NC + (g + 1) + FREE)
                    if g >= 2:
                        pe.wait_ge(x2_ready, b * NC + (g - 1) + FREE)
                    if g == 1:
                        pe.wait_ge(pooled_ready, b + FREE)
                    for t in range(4):
                        ins = pe.transpose(bank[3 + g % 2][:, t * 128:(t + 1) * 128],
                                           Y[:, t // 2, k * IH + 2 * cc + t % 2, :], ident[:, :])
                    ins.then_inc(x2_tr, 1)

                def logits(g):
                    k, cc = g // 2, g % 2
                    pe.wait_ge(x2_ready, b * NC + (g + 1) + FREE)
                    if cc == 0:
                        pe.wait_ge(ls_ready, b * NG + max(k - 1, 0) + FREE)
                    for t in range(4):
                        c = (t // 2) * IH + 2 * cc + t % 2
                        ins = pe.matmul(bank[5 + k % 2][:, c * E:(c + 1) * E], x2[:, g % 2, t * 128:(t + 1) * 128], gwT[:, :],
                                        start=True, stop=True)
                    ins.then_inc(logit_done, 1)

                def logits_T(k):
                    pe.wait_ge(ls_ready, b * NG + (k + 1) + FREE)
                    pe.wait_ge(l_ready, b * NG + k + FREE)
                    for i in range(IH):
                        ins = pe.transpose(bank[7][:, i * 128:(i + 1) * 128], Ls[:, k % 2, i].rearrange("p h e -> p (h e)"), ident[:, :])
                    ins.then_inc(lT_done, 1)

                for g in range(2, NC + 6):
                    if g < NC:
                        conv(b, g)
                    if 2 <= g < NC + 2:
                        x2_back(g - 2)
                    if 3 <= g < NC + 3:
                        logits(g - 3)
                    if g == NC + 3 and more:
                        for k in range(EARLY):
                            xT_tiles(b + 1, k)
                    if g % 2 == 1 and g >= 7:
                        logits_T((g - 7) // 2)

            before(0, 0)
            matrix(0)
            conv(0, 0)
            conv(0, 1)
            with pe.Fori(0, B - 1) as b:
                after(b, True)
                before(b + 1, EARLY)
                pe.wait_ge(l_ready, b * NG + NG + FREE)
                matrix(b + 1)
                conv(b + 1, 0)
                conv(b + 1, 1)
                pool_rows(b)
            after(B - 1, False)
            pool_rows(B - 1)

            pe.wait_ge(pooled_ready, B + FREE)
            pe.wait_ge(b_loaded, 48)

            def up(kk, s):
                q = kk * NW + s
                pe.wait_ge(w_loaded[s], kk * 32 + 32)
                pe.wait_ge(gelu_done[(s + 2) % NW], kk + (s >= 2) + FREE)
                for hc in range(HC):
                    dst = bank[s % 2][:, hc * EQ * B:(hc + 1) * EQ * B]
                    pe.matmul(dst.rearrange("p (e b) -> p e b", e=EQ), W1b[:, hc::HC],
                              ident[0:E, bass.ds(q * EQ, EQ)].unsqueeze(2).to_broadcast([E, EQ, B]), start=True, stop=False)
                    for i in range(EQ):
                        pv = pooled[:, :, bass.ds(q * EQ + i, 1)].rearrange("p b e -> p (b e)")
                        ins = pe.matmul(dst[:, i * B:(i + 1) * B], W1[s][:, i, hc::HC], pv, start=False, stop=(i == EQ - 1))
                ins.then_inc(up_done[s], 1)

            def down(kk, s):
                pe.wait_ge(gelu_done[s], kk + 1 + FREE)
                pe.wait_ge(o_ready[(s + 2) % NW], kk + (s >= 2) + FREE)
                for i in range(EQ):
                    dst = bank[2 + s % 2][0:B, i * O:(i + 1) * O]
                    for hc in range(HC):
                        ins = pe.matmul(dst, hT[s % 2][:, hc, i, :], W2[s][:, i, hc, :], start=(hc == 0), stop=(hc == HC - 1))
                ins.then_inc(down_done[s], 1)

            up(0, 0)
            with pe.Fori(0, NK - 1) as kk:
                for s in range(NW):
                    up(kk + (s + 1) // NW, (s + 1) % NW)
                    down(kk, s)
            for s in range(NW):
                if s < NW - 1:
                    up(NK - 1, s + 1)
                down(NK - 1, s)

            for s in range(NW):
                pe.wait_ge(o_ready[s], NK + FREE)
            with pe.Fori(0, B) as b:
                pe.wait_ge(ob_ready, b + 1)
                for j in range(NJ):
                    pe.wait_ge(blk_loaded[j], b * 32 + 32)
                    for q in range(NQ):
                        h, c0 = q // 4, (q % 4) * 512
                        pe.wait_ge(ev[q], b * NJ + j + FREE)
                        pe.matmul(bank[q][:, :], Ob[h], pin[j][:, c0:c0 + 512], start=True, stop=False)
                        for t in range(4):
                            ins = pe.matmul(bank[q][:, t * 128:(t + 1) * 128], xin[j][:, h, (q % 4) * 4 + t, :], ident[:, :],
                                            is_transpose=True, start=False, stop=(t == 3))
                        ins.then_inc(blk_used[j] if q == NQ - 1 else sc_done, 1)


_INS = ['x', 'L0_conv_w', 'L0_ffn_gate_w', 'L0_ffn_gate_b', 'L0_ffn_weight1', 'L0_ffn_weight2']


def kernel(**inputs):
    import numpy as _np
    import concourse.bacc as _bacc
    from concourse import mybir as _mybir
    from concourse.bass_utils import run_bass_kernel_spmd as _run

    nc = _bacc.Bacc("TRN2", target_bir_lowering=False, num_devices=1)
    arrays, args = {}, []
    for name in _INS:
        a = _np.ascontiguousarray(inputs[name])
        if name == 'x':
            a = a.reshape(B, C, N)
        arrays[f"in_{name}_dram"] = a
        args.append(nc.dram_tensor(f"in_{name}_dram", a.shape, _mybir.dt.from_np(a.dtype), kind="ExternalInput").ap())
    o = nc.dram_tensor("out_0_dram", (B, C, N), _mybir.dt.float32, kind="ExternalOutput").ap()
    build(nc, *args, o)
    r = _run(nc, [arrays], core_ids=[0])
    return r.results[0]["out_0_dram"].reshape(B, C, 128, 128)
```
